# Optimizing a Trainium2 kernel written in Bass

```python
import numpy as np
import jax
import jax.numpy as jnp

def _softmax(x, axis=-1):
    return jax.nn.softmax(x, axis=axis)

def _gelu(x):
    return jax.nn.gelu(x, approximate=True)

def _silu(x):
    return jax.nn.silu(x)

def _sigmoid(x):
    return jax.nn.sigmoid(x)

def _layernorm(x, axis=-1, eps=1e-05):
    m = jnp.mean(x, axis=axis, keepdims=True)
    v = jnp.var(x, axis=axis, keepdims=True)
    return (x - m) / jnp.sqrt(v + eps)

def _scatter_add(tgt, idx, src, axis=0):
    return tgt.at[idx].add(src)

def _segment_sum(src, seg, n):
    return jax.ops.segment_sum(src, seg, n)
kernel_name = 'mk_prb_d1_jaxref_r4_f7dfc9'

def setup_inputs(seed: int=0):
    np.random.seed(seed)
    _w = jnp.asarray

    def _L0_attn_setup():
        import jax, jax.numpy as jnp
        import numpy as np
        B, S, D, H = (2, 512, 512, 16)
        HD = D // H

        def _alibi_slopes(num_heads):
            ratio = 2.0 ** (-8.0 / num_heads)
            return ratio ** jnp.arange(1, num_heads + 1, dtype=jnp.float32)
        key = jax.random.key(seed)
        ks = jax.random.split(key, 9)
        sd = 1.0 / np.sqrt(D)
        inp = {'x': jax.random.normal(ks[0], (B, S, D), dtype=jnp.float32)}
        for i, name in enumerate(['Wq', 'Wk', 'Wv', 'Wo']):
            inp[name] = jax.random.normal(ks[1 + i], (D, D), dtype=jnp.float32) * sd
        for i, name in enumerate(['bq', 'bk', 'bv', 'bo']):
            inp[name] = jax.random.normal(ks[5 + i], (D,), dtype=jnp.float32) * 0.02
        return inp
    _L0_attn_in = _L0_attn_setup()

    def _L0_ffn_setup():
        import jax, jax.numpy as jnp
        import numpy as np
        E = 8
        TOP_K = 2
        D = 512
        F_E = 2048 // E
        EPS = 1e-06
        SCALE = E / TOP_K
        key = jax.random.key(seed)
        ks = jax.random.split(key, 6)
        B, S = (2, 512)
        std = 0.02
        return {'hidden_states': jax.random.normal(ks[0], (B, S, D), jnp.float32), 'router_w': jax.random.normal(ks[1], (E, D), jnp.float32) * std, 'norm_w': jnp.ones((D,), jnp.float32), 'gate_w': jax.random.normal(ks[2], (E, D, F_E), jnp.float32) * std, 'up_w': jax.random.normal(ks[3], (E, D, F_E), jnp.float32) * std, 'down_w': jax.random.normal(ks[4], (E, F_E, D), jnp.float32) * std}
    _L0_ffn_in = _L0_ffn_setup()
    _d = {'L0_attn_x': _L0_attn_in['x'], 'L0_attn_Wq': _L0_attn_in['Wq'], 'L0_attn_bq': _L0_attn_in['bq'], 'L0_attn_Wk': _L0_attn_in['Wk'], 'L0_attn_bk': _L0_attn_in['bk'], 'L0_attn_Wv': _L0_attn_in['Wv'], 'L0_attn_bv': _L0_attn_in['bv'], 'L0_attn_Wo': _L0_attn_in['Wo'], 'L0_attn_bo': _L0_attn_in['bo'], 'L0_ffn_router_w': _L0_ffn_in['router_w'], 'L0_ffn_norm_w': _L0_ffn_in['norm_w'], 'L0_ffn_gate_w': _L0_ffn_in['gate_w'], 'L0_ffn_up_w': _L0_ffn_in['up_w'], 'L0_ffn_down_w': _L0_ffn_in['down_w']}
    _x0 = _d['L0_attn_x']
    _d['L0_attn_x'] = jax.random.normal(jax.random.fold_in(jax.random.key(seed), 1), (2, 2048, 512), dtype=_x0.dtype)
    del _x0
    return _d

def reference(L0_attn_x, L0_attn_Wq, L0_attn_bq, L0_attn_Wk, L0_attn_bk, L0_attn_Wv, L0_attn_bv, L0_attn_Wo, L0_attn_bo, L0_ffn_router_w, L0_ffn_norm_w, L0_ffn_gate_w, L0_ffn_up_w, L0_ffn_down_w):

    def _L0_attn_ref(x, Wq, bq, Wk, bk, Wv, bv, Wo, bo):
        import jax, jax.numpy as jnp
        import numpy as np
        B, S, D, H = (2, 512, 512, 16)
        HD = D // H

        def _alibi_slopes(num_heads):
            ratio = 2.0 ** (-8.0 / num_heads)
            return ratio ** jnp.arange(1, num_heads + 1, dtype=jnp.float32)
        b, s, d = x.shape

        def proj(W, bias):
            return (x @ W + bias).reshape(b, s, H, HD).transpose(0, 2, 1, 3)
        q, k, v = (proj(Wq, bq), proj(Wk, bk), proj(Wv, bv))
        scores = jnp.einsum('bhqd,bhkd->bhqk', q, k) / jnp.sqrt(jnp.float32(HD))
        distances = jnp.arange(1 - s, 1, dtype=jnp.float32)
        bias = _alibi_slopes(H)[None, :, None, None] * distances[None, None, None, :]
        scores = scores + bias
        causal = jnp.tril(jnp.ones((s, s), dtype=bool))[None, None]
        scores = jnp.where(causal, scores, jnp.finfo(scores.dtype).min)
        attn = jax.nn.softmax(scores, axis=-1)
        ctx = jnp.einsum('bhqk,bhkd->bhqd', attn, v)
        ctx = ctx.transpose(0, 2, 1, 3).reshape(b, s, d)
        return ctx @ Wo + bo

    def _L0_ffn_ref(hidden_states, router_w, norm_w, gate_w, up_w, down_w):
        import jax, jax.numpy as jnp
        import numpy as np
        E = 8
        TOP_K = 2
        D = 512
        F_E = 2048 // E
        EPS = 1e-06
        SCALE = E / TOP_K
        B, S, Dm = hidden_states.shape
        T = B * S
        flat = hidden_states.reshape(T, Dm)
        xf = flat.astype(jnp.float32)
        var = jnp.mean(xf * xf, axis=-1, keepdims=True)
        router_in = norm_w * (xf * jax.lax.rsqrt(var + EPS)).astype(flat.dtype)
        logits = router_in @ router_w.T
        probs = jax.nn.softmax(logits, axis=-1)
        topw, topi = jax.lax.top_k(probs, TOP_K)
        topw = topw / jnp.sum(topw, axis=-1, keepdims=True)
        cw = jnp.zeros((T, E), flat.dtype).at[jnp.arange(T)[:, None], topi].add(topw)
        g = jnp.einsum('td,edf->tef', flat, gate_w)
        u = jnp.einsum('td,edf->tef', flat, up_w)
        a = jax.nn.silu(g) * u
        expert_out = jnp.einsum('tef,efd->ted', a, down_w)
        y = jnp.einsum('ted,te->td', expert_out, cw) * SCALE
        return y.reshape(B, S, Dm)
    x = L0_attn_x
    xn = _layernorm(x, axis=-1)
    x = x + _L0_attn_ref(xn, L0_attn_Wq, L0_attn_bq, L0_attn_Wk, L0_attn_bk, L0_attn_Wv, L0_attn_bv, L0_attn_Wo, L0_attn_bo) + _L0_ffn_ref(xn, L0_ffn_router_w, L0_ffn_norm_w, L0_ffn_gate_w, L0_ffn_up_w, L0_ffn_down_w)
    return x

_drawn_inputs = setup_inputs


def setup_inputs(seed=0):
    import zlib

    import numpy as np

    out = dict(_drawn_inputs(seed))
    spreads = {'L0_ffn_norm_w': (1.0, 0.2)}
    factors = {'L0_attn_bq': 8.0, 'L0_attn_bk': 8.0, 'L0_attn_bv': 3.213, 'L0_attn_bo': 3.144}
    for name, (base, spread) in spreads.items():
        noise = np.random.default_rng([zlib.crc32(name.encode()), seed]).standard_normal(out[name].shape)
        drawn = base * np.exp(spread * noise) if base else spread * noise
        out[name] = jnp.asarray(drawn.astype(out[name].dtype))
    for name, factor in factors.items():
        out[name] = (out[name] * factor).astype(out[name].dtype)
    return out
```

```python
from contextlib import ExitStack

import concourse.bass as bass
from concourse import mybir

F32 = mybir.dt.float32
F32R = mybir.dt.float32r
BF16 = mybir.dt.bfloat16
I32 = mybir.dt.int32
U32 = mybir.dt.uint32
ACT = mybir.ActivationFunctionType
ALU = mybir.AluOpType
AX = mybir.AxisListType

P = 128
B, S, D, H = 2, 2048, 512, 16
HD = D // H
E, TOP_K = 8, 2
F = 2048 // E
T = B * S
TT = T // P
QT = S // P
KD = D // P
KF = F // P
CH = 512
TPC = CH // P
NCH = T // CH
G = D // P
HPG = P // HD
NH = B * H
NMT = (TOP_K * T + E * (P - 1)) // P
LN_EPS, RMS_EPS = 1e-5, 1e-6
MOE_SCALE = E / TOP_K
SCALE = float(HD) ** -0.5
NEG = -float(2 ** 100)

ROW_BIAS, ROW_MAX, ROWS = 96, 98, 100

S_UNITS = [(qc, kt) for qc in range(S // CH) for kt in range(TPC * (qc + 1))]
NS = len(S_UNITS)
M_WIDE = 1024
M_UNITS = [(qt, half) for qt in range(QT) for half in range((qt * P) // M_WIDE + 1)]
NM = len(M_UNITS)
M_SLOTS = NM + 1


def s_span(u):
    qc, kt = S_UNITS[u]
    q0 = max(CH * qc, P * kt)
    return q0, CH * (qc + 1) - q0


def m_span(m):
    qt, half = M_UNITS[m]
    k0 = half * M_WIDE
    return k0, min((qt + 1) * P, k0 + M_WIDE) - k0


LAST_UNIT = [max(u for u in range(NS) if S_UNITS[u][0] == qc) for qc in range(S // CH)]
SPLIT = [kt % 3 != 2 and s_span(u)[1] > P for u, (qc, kt) in enumerate(S_UNITS)]
NSPLIT = sum(SPLIT)
PV_LAG = 3
LOW_LAG = 1


def attend_order():
    total, m_total = sum(s_span(u)[1] for u in range(NS)), sum(m_span(m)[1] for m in range(NM))
    order, m, done, m_done, w_at = [], 0, 0, 0, None
    for u in range(NS + PV_LAG):
        if u < NS:
            order.append(("S", u))
            done += s_span(u)[1]
        if 0 <= u - LOW_LAG < NS and SPLIT[u - LOW_LAG]:
            order.append(("L", u - LOW_LAG))
        while m < NM and m_done <= done / (0.85 * total) * m_total:
            order.append(("M", m))
            m_done += m_span(m)[1]
            m += 1
            if m == NM:
                order.append(("X", 0))
                w_at = u + 2
        if u == w_at:
            order.append(("W", 0))
        if u >= PV_LAG:
            order.append(("V", u - PV_LAG))
        for qc, last in enumerate(LAST_UNIT):
            if u == min(last + PV_LAG + 1, NS + PV_LAG - 1):
                order.append(("O", qc))
    return order


ATTEND = attend_order()
HEADS_RING = 3
P_RING = 4
VS = 3 * HD


STEPS_PER_PAIR = 34


class Links:

    def __init__(self, eng, sem):
        self.eng, self.sem, self.base, self.n = eng, sem, 0, 0

    def __call__(self, ins):
        self.n += 1
        ins.then_inc(self.sem, 1)
        self.eng.wait_ge(self.sem, self.base + self.n)


def attention_and_experts(nc, x, Wq, bq, Wk, bk, Wv, bv, Wo, bo, rwT, nw, gate_w, up_w, down_w,
                          cst, rows, alibi, spread, token_pairs, no_pairs, no_rows, out):
    with ExitStack() as top:
        def dram(name, shape, dt):
            return nc.dram_tensor(name, shape, dt).ap()

        q_hi_d, q_lo_d = dram("q_hi_d", [B, D, S], F32), dram("q_lo_d", [B, D, S], F32)
        k_hi_d, k_lo_d = dram("k_hi_d", [B, D, S], F32), dram("k_lo_d", [B, D, S], F32)
        ctx_d = dram("ctx_d", [B * D, S], F32)
        weight_sums_d = dram("weight_sums_d", [NH, S], F32)
        inverse_d = dram("inverse_d", [2, NH, S], F32)
        bias_d = dram("bias_d", [H, 2, S], F32)
        xn_d = dram("xn_d", [T + P, D], F32)
        list_d = dram("list_d", [NMT * P, 2], I32)

        def sb(ctx, name, shape, dt):
            return ctx.enter_context(nc.sbuf_tensor(name, shape, dt))

        def ps(ctx, name, shape, dt=F32):
            return ctx.enter_context(nc.psum_tensor(name, shape, dt))

        def sem(ctx, name):
            return ctx.enter_context(nc.semaphore(name))

        consts = sb(top, "consts", [P, 5, P], F32)
        ident, triu, ones = consts[:, 0, :], consts[:, 3, :], consts[:, 4, :]
        mask_r = sb(top, "mask_r", [P, 3, P], BF16)
        ident_r, mask_m, mask_s = mask_r[:, 0, :], mask_r[:, 1, :], mask_r[:, 2, :]
        rows_c = sb(top, "rows_c", [P, E + NMT + 1], F32)
        top_val = sb(top, "top_val", [P, TT, 8], F32)
        top_idx = sb(top, "top_idx", [P, TT, 8], U32)
        slot = sb(top, "slot", [P, TT, TOP_K], U32)
        tile_expert = sb(top, "tile_expert", [1, NMT + 1], I32)

        with ExitStack() as early:
            values = sb(early, "values", [P, TT * D], F32)
            project(nc, sb, ps, sem, locals())
            attend(nc, sb, ps, sem, locals())
        with ExitStack() as late:
            w_hi = sb(late, "gu_hi", [P, E, KD, 2 * F], F32R)
            w_lo = sb(late, "gu_lo", [P, E, KD, 2 * F], F32R)
            output(nc, sb, ps, sem, locals())
            experts(nc, sb, ps, sem, locals())



def project(nc, sb, ps, sem, t):
    x = t["x"]
    consts, mask_r, ident = t["consts"], t["mask_r"], t["ident"]
    values, top_val, top_idx = t["values"], t["top_val"], t["top_idx"]
    NJ = 2 * G + TPC
    BANKS = 4
    QK_RING = 4
    with ExitStack() as ctx:
        w_raw = sb(ctx, "w_raw", [P, KD, D], F32)
        w_hi = sb(ctx, "w_hi", [P, 3, KD, D], F32R)
        w_lo = sb(ctx, "w_lo", [P, 3, KD, D], F32R)
        rw_raw = sb(ctx, "rw_raw", [P, KD, E], F32)
        nw_col = sb(ctx, "nw_col", [P, KD], F32)
        rw = sb(ctx, "rw", [P, KD, 2 * E], F32R)
        b_col = sb(ctx, "b_col", [P, 2, G], F32)
        bv_row = sb(ctx, "bv_row", [P, D], F32)
        al_raw = sb(ctx, "al_raw", [H, CH], F32)
        al = sb(ctx, "al", [H, 2, CH], F32R)
        xs = sb(ctx, "xs", [P, 2, TPC, D], F32)
        x_hi = sb(ctx, "x_hi", [P, 2, KD, CH], F32R)
        x_lo = sb(ctx, "x_lo", [P, 2, KD, CH], F32R)
        qk_hi = sb(ctx, "qk_hi", [P, QK_RING, CH], F32R)
        qk_lo = sb(ctx, "qk_lo", [P, QK_RING, CH], F32R)
        squares = sb(ctx, "squares", [P, D], F32)
        stats = sb(ctx, "stats", [P, TPC, 6], F32)
        mv = sb(ctx, "mv", [P, TPC, 2], F32)
        ve = sb(ctx, "ve", [P, TPC], F32)
        sd = sb(ctx, "sd", [P, TPC], F32)
        rstd = sb(ctx, "rstd", [P, TPC], F32)
        newton = sb(ctx, "newton", [P, TPC], F32)
        ssq = sb(ctx, "ssq", [P, TPC], F32)
        ms = sb(ctx, "ms", [P, TPC], F32)
        rsd = sb(ctx, "rsd", [P, TPC], F32)
        rms = sb(ctx, "rms", [P, 2, TPC], F32)
        halves = sb(ctx, "halves", [P, TPC, 2 * E], F32)
        logits = sb(ctx, "logits", [P, TPC, E], F32)
        pad = sb(ctx, "pad", [P, 1], F32)
        best = sb(ctx, "best", [P, TPC, 8], F32)
        best_at = sb(ctx, "best_at", [P, TPC, 8], U32)
        xt = ps(ctx, "xt", [P, 2, CH])
        pj = ps(ctx, "pj", [P, BANKS, CH])
        pr = ps(ctx, "pr", [P, CH])

        small_loaded = sem(ctx, "small_loaded")
        w_raw_loaded = sem(ctx, "w_raw_loaded")
        w_hi_done = sem(ctx, "w_hi_done")
        w_split = sem(ctx, "w_split")
        rw_ready = sem(ctx, "rw_ready")
        x_loaded = [sem(ctx, f"x_loaded{p}") for p in range(2)]
        ve_ready = sem(ctx, "ve_ready")
        sd_ready = sem(ctx, "sd_ready")
        xn_ready = sem(ctx, "xn_ready")
        ssq_ready = sem(ctx, "ssq_ready")
        ms_ready = sem(ctx, "ms_ready")
        rsd_ready = sem(ctx, "rsd_ready")
        xt_ready = sem(ctx, "xt_ready")
        xh_ready = sem(ctx, "xh_ready")
        xl_ready = sem(ctx, "xl_ready")
        pj_ready = sem(ctx, "pj_ready")
        qk_hi_ready = sem(ctx, "qk_hi_ready")
        pj_used = sem(ctx, "pj_used")
        r_ready = sem(ctx, "r_ready")
        r_used = sem(ctx, "r_used")
        xn_stored = [sem(ctx, f"xn_stored{p}") for p in range(2)]
        qk_stored = [sem(ctx, f"qk_stored{p}") for p in range(QK_RING)]
        al_loaded = sem(ctx, "al_loaded")
        al_hi_ready = sem(ctx, "al_hi_ready")
        al_ready = sem(ctx, "al_ready")
        al_stored = sem(ctx, "al_stored")
        dve_step = sem(ctx, "dve_step")
        N_SMALL = 10
        block = ctx.enter_context(nc.Block())

        def x_rows(c):
            return x[bass.ds(c * CH, CH), :].rearrange("(j p) d -> p j d", p=P)

        @block.sync
        def _(sp):
            sp.dma_start(xs[:, 0], x_rows(0)).then_inc(x_loaded[0], 16)
            for dst, src in ((consts[:, :, :], t["cst"].rearrange("p (a n) -> p a n", a=5)),
                             (rw_raw[:, :, :], t["rwT"].rearrange("p (k e) -> p k e", k=KD)),
                             (nw_col[:, :], t["nw"]),
                             (b_col[:, 0], t["bq"]),
                             (b_col[:, 1], t["bk"]),
                             (bv_row[:, :], t["bv"].partition_broadcast(P)),
                             (t["rows_c"][:, :], t["rows"]),
                             (t["list_d"].rearrange("(p n) o -> p (n o)", p=P), t["no_pairs"]),
                             (t["xn_d"][T:T + P, :], t["no_rows"]),
                             (t["out"][T:T + P, :], t["no_rows"])):
                sp.dma_start(dst, src).then_inc(small_loaded, 16)
            for w, name in enumerate(("Wq", "Wk", "Wv")):
                if w:
                    sp.wait_ge(w_split, w)
                sp.dma_start(w_raw[:, :, :], t[name].rearrange("(k p) n -> p k n", p=P)).then_inc(w_raw_loaded, 16)
                if w == 0:
                    sp.dma_start(xs[:, 1], x_rows(1)).then_inc(x_loaded[1], 16)
            for a in range(S // CH):
                if a:
                    sp.wait_ge(al_ready, a)
                sp.dma_start(al_raw[:, :], t["alibi"][:, a * CH:(a + 1) * CH]).then_inc(al_loaded, 16)
                sp.wait_ge(al_ready, a + 1)
                sp.dma_start(t["bias_d"][:, :, a * CH:(a + 1) * CH], al[:, :, :].bitcast(F32)).then_inc(al_stored, 16)

            def chunk(c, par, load):
                sp.wait_ge(xn_ready, TPC * (c + 1))
                sp.dma_start(t["xn_d"][bass.ds(c * CH, CH), :].rearrange("(j p) d -> p j d", p=P),
                             xs[:, par]).then_inc(xn_stored[par], 16)
                for g in range(2 * G):
                    sp.wait_ge(pj_used, BANKS + NJ * c + g + 1)
                    hi_d, lo_d = (t["q_hi_d"], t["q_lo_d"]) if g < G else (t["k_hi_d"], t["k_lo_d"])
                    rows = slice((g % G) * P, (g % G + 1) * P)
                    cols = bass.ds((c % (NCH // B)) * CH, CH)
                    for d, s in ((hi_d, qk_hi), (lo_d, qk_lo)):
                        dst = d[bass.ds(c // (NCH // B), 1), rows, cols].rearrange("a r n -> (a r) n")
                        sp.dma_start(dst, s[:, g % QK_RING].bitcast(F32)).then_inc(qk_stored[g % QK_RING], 16)
                    if load and g == 0:
                        sp.wait_ge(ssq_ready, 1 + TPC * (c + 1))
                        sp.wait_ge(xt_ready, KD * (c + 1))
                        sp.wait_ge(xn_stored[par], 16 * (c // 2 + 1))
                        sp.dma_start(xs[:, par], x_rows(c + 2)).then_inc(x_loaded[par], 16)

            with nc.sync.Fori(0, NCH // 2 - 1) as i:
                chunk(2 * i, 0, True)
                chunk(2 * i + 1, 1, True)
            chunk(NCH - 2, 0, False)
            chunk(NCH - 1, 1, False)
            sp.wait_ge(small_loaded, 16 * N_SMALL)
            sp.wait_ge(al_stored, 16 * (S // CH))
            for p in range(2):
                sp.wait_ge(xn_stored[p], 16 * NCH // 2)
            for p in range(QK_RING):
                sp.wait_ge(qk_stored[p], 32 + 32 * 2 * G // QK_RING * NCH)

        @block.gpsimd
        def _(pool):
            for a in range(S // CH):
                pool.wait_ge(al_loaded, 16 * (a + 1))
                if a:
                    pool.wait_ge(al_stored, 16 * a)
                nc.gpsimd.tensor_copy(al[:, 0], al_raw[:, :]).then_inc(al_hi_ready, 1)
                pool.wait_ge(al_hi_ready, a + 1)
                nc.gpsimd.tensor_tensor(al[:, 1], al_raw[:, :], al[:, 0].bitcast(F32), ALU.subtract).then_inc(al_ready, 1)

        @block.scalar
        def _(act):
            def w_high(w):
                act.wait_ge(w_raw_loaded, 16 * (w + 1))
                nc.scalar.activation(w_hi[:, w], w_raw[:, :, :], ACT.Copy).then_inc(w_hi_done, 1)

            def deviation(c):
                act.wait_ge(ve_ready, c + 1)
                nc.scalar.activation(sd[:, :], ve[:, :], ACT.Sqrt).then_inc(sd_ready, 1)

            def square_sums(c, par):
                for j in range(TPC):
                    act.wait_ge(xn_ready, TPC * c + j + 1)
                    act.wait_ge(ssq_ready, TPC * c + j + 1)
                    nc.scalar.activation(squares[:, :], xs[:, par, j], ACT.Square,
                                         accum_out=ssq[:, j:j + 1]).then_inc(ssq_ready, 1)

            def router_root(c):
                act.wait_ge(ms_ready, c + 1)
                nc.scalar.activation(rsd[:, :], ms[:, :], ACT.Sqrt).then_inc(rsd_ready, 1)

            def x_high(c, par, k):
                act.wait_ge(xt_ready, KD * c + k + 1)
                nc.scalar.activation(x_hi[:, par, k], xt[:, k % 2], ACT.Copy).then_inc(xh_ready, 1)

            def qk_high(c, g):
                act.wait_ge(pj_ready, NJ * c + g + 1)
                act.wait_ge(qk_stored[g % QK_RING], 32 * (2 * G // QK_RING * c + g // QK_RING + 1))
                nc.scalar.activation(qk_hi[:, g % QK_RING], pj[:, g % BANKS], ACT.Identity,
                                     bias=b_col[:, g // G, g % G:g % G + 1]).then_inc(qk_hi_ready, 1)

            act.sem_inc(ssq_ready, 1)
            for p in range(QK_RING):
                act.sem_inc(qk_stored[p], 32)
            deviation(0)
            square_sums(0, 0)
            router_root(0)
            act.wait_ge(small_loaded, 16 * N_SMALL)
            w_high(0)
            for k in range(KD):
                x_high(0, 0, k)
            w_high(1)
            w_high(2)

            def chunk(c, par, ahead):
                for g in range(2 * G):
                    if ahead and g >= G:
                        x_high(c + 1, 1 - par, g - G)
                    qk_high(c, g)
                    if ahead and g == 0:
                        deviation(c + 1)
                    if ahead and g == 2:
                        square_sums(c + 1, 1 - par)
                    if ahead and g == G:
                        router_root(c + 1)

            with nc.scalar.Fori(0, NCH // 2 - 1) as i:
                chunk(2 * i, 0, True)
                chunk(2 * i + 1, 1, True)
            chunk(NCH - 2, 0, True)
            chunk(NCH - 1, 1, False)

        @block.vector
        def _(dve):
            step = Links(dve, dve_step)

            def inverse_root(out, var, root):
                step(nc.vector.reciprocal(out, root))
                step(nc.vector.tensor_tensor(newton[:, :], out, out, ALU.mult))
                step(nc.vector.tensor_tensor(newton[:, :], newton[:, :], var, ALU.mult))
                step(nc.vector.tensor_scalar(newton[:, :], newton[:, :], -0.5, 1.5, ALU.mult, ALU.add))
                step(nc.vector.tensor_tensor(out, out, newton[:, :], ALU.mult))

            def norm_stats(c, par):
                dve.wait_ge(x_loaded[par], 16 * (c // 2 + 1))
                for j in range(TPC):
                    last = nc.vector.bn_stats(stats[:, j], xs[:, par, j])
                step(last)
                nc.vector.memset(pad[:, :], 0.0)
                for j in range(TPC):
                    last = nc.vector.bn_aggr(mv[:, j], stats[:, j])
                step(last)
                nc.vector.tensor_scalar(ve[:, :], mv[:, :, 1], LN_EPS, None, ALU.add).then_inc(ve_ready, 1)

            def normalise(c, par):
                dve.wait_ge(sd_ready, c + 1)
                inverse_root(rstd[:, :], ve[:, :], sd[:, :])
                for j in range(TPC):
                    nc.vector.tensor_scalar(xs[:, par, j], xs[:, par, j], mv[:, j, 0:1], rstd[:, j:j + 1],
                                            ALU.subtract, ALU.mult).then_inc(xn_ready, 1)

            def mean_square(c):
                dve.wait_ge(ssq_ready, 1 + TPC * (c + 1))
                nc.vector.tensor_scalar(ms[:, :], ssq[:, :], 1.0 / D, RMS_EPS, ALU.mult, ALU.add).then_inc(ms_ready, 1)

            def router_scale(c, par):
                dve.wait_ge(rsd_ready, c + 1)
                inverse_root(rms[:, par], ms[:, :], rsd[:, :])

            def w_low(w):
                dve.wait_ge(w_hi_done, w + 1)
                nc.vector.tensor_tensor(w_lo[:, w], w_raw[:, :, :], w_hi[:, w].bitcast(F32),
                                        ALU.subtract).then_inc(w_split, 1)

            def x_low(c, par, k):
                dve.wait_ge(xh_ready, KD * c + k + 1)
                nc.vector.tensor_tensor(x_lo[:, par, k], xt[:, k % 2], x_hi[:, par, k].bitcast(F32),
                                        ALU.subtract).then_inc(xl_ready, 1)

            def qk_low(c, g):
                dve.wait_ge(qk_hi_ready, 2 * G * c + g + 1)
                nc.vector.scalar_tensor_tensor(qk_lo[:, g % QK_RING], pj[:, g % BANKS], b_col[:, g // G, g % G:g % G + 1],
                                               qk_hi[:, g % QK_RING].bitcast(F32), ALU.add,
                                               ALU.subtract).then_inc(pj_used, 1)

            def keep_values(c, j):
                dve.wait_ge(pj_ready, NJ * c + 2 * G + j + 1)
                nc.vector.tensor_tensor(values[:, bass.ds((TPC * c + j) * D, D)], pj[:, j % BANKS], bv_row[:, :],
                                        ALU.add).then_inc(pj_used, 1)

            def route(c, par):
                dve.wait_ge(r_ready, c + 1)
                nc.vector.tensor_copy(halves[:, :, :], pr[:, 0:TPC * 2 * E].rearrange("p (j e) -> p j e", j=TPC)).then_inc(r_used, 1)
                dve.wait_ge(r_used, c + 2)
                step(nc.vector.tensor_tensor(logits[:, :, :], halves[:, :, 0:E], halves[:, :, E:2 * E], ALU.add))
                step(nc.vector.tensor_tensor(logits[:, :, :], logits[:, :, :],
                                             rms[:, par].unsqueeze(2).to_broadcast([P, TPC, E]), ALU.mult))
                nc.vector.memset(pad[:, :], 0.0)
                for j in range(TPC):
                    last = nc.vector.max(best[:, j], logits[:, j])
                step(last)
                nc.vector.memset(pad[:, :], 0.0)
                for j in range(TPC):
                    last = nc.vector.max_index(best_at[:, j], best[:, j], logits[:, j])
                step(last)
                nc.vector.tensor_copy(top_val[:, bass.ds(TPC * c, TPC), :], best[:, :, :])
                step(nc.vector.tensor_copy(top_idx[:, bass.ds(TPC * c, TPC), :], best_at[:, :, :]))

            dve.sem_inc(xl_ready, 2)
            dve.sem_inc(pj_used, BANKS)
            dve.sem_inc(r_used, 1)
            norm_stats(0, 0)
            normalise(0, 0)
            mean_square(0)
            dve.wait_ge(small_loaded, 16 * N_SMALL)
            nc.vector.tensor_copy(mask_r[:, :, :], consts[:, 0:3, :])
            for k in range(KD):
                last = nc.vector.tensor_scalar(rw_raw[:, k], rw_raw[:, k], nw_col[:, k:k + 1], None, ALU.mult)
            step(last)
            step(nc.vector.tensor_copy(rw[:, :, 0:E], rw_raw[:, :, :]))
            nc.vector.tensor_tensor(rw[:, :, E:2 * E], rw_raw[:, :, :], rw[:, :, 0:E].bitcast(F32),
                                    ALU.subtract).then_inc(rw_ready, 1)
            router_scale(0, 0)
            w_low(0)
            for k in range(KD):
                x_low(0, 0, k)
            w_low(1)
            w_low(2)

            def chunk(c, par, ahead):
                if ahead:
                    norm_stats(c + 1, 1 - par)
                for g in range(2 * G):
                    if ahead and g >= G:
                        x_low(c + 1, 1 - par, g - G)
                    qk_low(c, g)
                    if ahead and g == 0:
                        normalise(c + 1, 1 - par)
                    if ahead and g == G - 1:
                        mean_square(c + 1)
                    if ahead and g == G:
                        router_scale(c + 1, 1 - par)
                for j in range(TPC):
                    keep_values(c, j)
                route(c, par)

            start = step.n
            with nc.vector.Fori(0, NCH // 2 - 1) as i:
                step.base, step.n = start + i * STEPS_PER_PAIR, 0
                chunk(2 * i, 0, True)
                chunk(2 * i + 1, 1, True)
                assert step.n == STEPS_PER_PAIR, step.n
            step.base, step.n = start + (NCH // 2 - 1) * STEPS_PER_PAIR, 0
            chunk(NCH - 2, 0, True)
            chunk(NCH - 1, 1, False)

        @block.tensor
        def _(pe):
            def transpose_x(c, par, k):
                pe.wait_ge(xn_ready, TPC * (c + 1))
                pe.wait_ge(xl_ready, KD * c + k + 1)
                for j in range(TPC):
                    last = nc.tensor.transpose(xt[:, k % 2, j * P:(j + 1) * P], xs[:, par, j, k * P:(k + 1) * P], ident)
                last.then_inc(xt_ready, 1)

            def tile(c, g, pairs):
                pe.wait_ge(pj_used, NJ * c + g + 1)
                for k in range(KD):
                    for n, (lhsT, rhs) in enumerate(pairs(k)):
                        last = nc.tensor.matmul(pj[:, g % BANKS], lhsT, rhs, start=(k == 0 and n == 0),
                                                stop=(k == KD - 1 and n == 2))
                last.then_inc(pj_ready, 1)

            def qk_tile(c, par, g):
                w, cols = g // G, slice((g % G) * P, (g % G + 1) * P)
                tile(c, g, lambda k: ((w_hi[:, w, k, cols], x_hi[:, par, k]), (w_hi[:, w, k, cols], x_lo[:, par, k]),
                                      (w_lo[:, w, k, cols], x_hi[:, par, k])))

            def v_tile(c, par, j):
                rows = slice(j * P, (j + 1) * P)
                tile(c, 2 * G + j, lambda k: ((x_hi[:, par, k, rows], w_hi[:, 2, k]), (x_hi[:, par, k, rows], w_lo[:, 2, k]),
                                              (x_lo[:, par, k, rows], w_hi[:, 2, k])))

            def router_tiles(c, par):
                pe.wait_ge(r_used, c + 1)
                for j in range(TPC):
                    rows = slice(j * P, (j + 1) * P)
                    for k in range(KD):
                        for n, part in enumerate((x_hi, x_lo)):
                            last = nc.tensor.matmul(pr[:, 2 * E * j:2 * E * (j + 1)], part[:, par, k, rows], rw[:, k],
                                                    start=(k == 0 and n == 0), stop=(k == KD - 1 and n == 1))
                last.then_inc(r_ready, 1)

            pe.wait_ge(small_loaded, 16 * N_SMALL)
            pe.wait_ge(rw_ready, 1)
            for k in range(KD):
                transpose_x(0, 0, k)

            def chunk(c, par, ahead):
                pe.wait_ge(xl_ready, 2 + KD * (c + 1))
                pe.wait_ge(w_split, 1)
                for g in range(2 * G):
                    if g == G:
                        pe.wait_ge(w_split, 2)
                    if ahead and g >= G:
                        transpose_x(c + 1, 1 - par, g - G)
                    qk_tile(c, par, g)
                pe.wait_ge(w_split, 3)
                for j in range(TPC):
                    v_tile(c, par, j)
                router_tiles(c, par)

            with nc.tensor.Fori(0, NCH // 2 - 1) as i:
                chunk(2 * i, 0, True)
                chunk(2 * i + 1, 1, True)
            chunk(NCH - 2, 0, True)
            chunk(NCH - 1, 1, False)


def attend(nc, sb, ps, sem, t):
    ident, ident_r, mask_m, mask_s = t["ident"], t["ident_r"], t["mask_m"], t["mask_s"]
    values = t["values"]
    with ExitStack() as ctx:
        k_st = sb(ctx, "k_st", [P, HEADS_RING, S], F32R)
        q_st = sb(ctx, "q_st", [P, HEADS_RING, S], F32R)
        v_split = sb(ctx, "v_split", [P, HEADS_RING, QT, VS], F32R)
        v_whole = sb(ctx, "v_whole", [P, HEADS_RING, QT, 2 * HD], F32)
        probs = sb(ctx, "probs", [P, P_RING, CH], F32)
        probs_hi = sb(ctx, "probs_hi", [P, P_RING, CH], F32R)
        probs_lo = sb(ctx, "probs_lo", [P, P_RING, CH], F32R)
        high_sums = sb(ctx, "high_sums", [2 * HD, 2, CH], F32)
        low_sums = sb(ctx, "low_sums", [HD, 2, CH], F32)
        m_part = sb(ctx, "m_part", [P, QT + QT // 2], F32)
        m_neg = sb(ctx, "m_neg", [P, QT], F32)
        m_rows = sb(ctx, "m_rows", [QT, 2, P], F32R)
        idx_f = sb(ctx, "idx_f", [P, TT, TOP_K], F32)
        hot = sb(ctx, "hot", [P, TOP_K, TT, E], F32)
        both = sb(ctx, "both", [P, TT, E], F32)
        counts = sb(ctx, "counts", [P, 2, TT, E], F32)
        so_far = sb(ctx, "so_far", [P, TT, E], F32)
        padded_i = sb(ctx, "padded_i", [P, E], I32)
        padded = sb(ctx, "padded", [P, E], F32)
        ends = sb(ctx, "ends", [P, E], F32)
        starts = sb(ctx, "starts", [P, E], F32)
        base = sb(ctx, "base", [P, TT, E], F32)
        slot_f = sb(ctx, "slot_f", [P, TT, TOP_K], F32)
        passed = sb(ctx, "passed", [1, NMT + 1, E], F32)
        te_f = sb(ctx, "te_f", [1, NMT + 1], F32)
        gap = sb(ctx, "gap", [P, TT], F32)
        ratio = sb(ctx, "ratio", [P, TT], F32)
        denom = sb(ctx, "denom", [P, TT], F32)
        pairs = sb(ctx, "pairs", [P, TT, TOP_K, 2], I32)

        m_ps = ps(ctx, "m_ps", [P, 2, M_WIDE])
        s_ps = ps(ctx, "s_ps", [P, 2, CH])
        o_ps = ps(ctx, "o_ps", [P, 2, CH])

        st_ones = sem(ctx, "st_ones")
        st_loaded = [sem(ctx, f"st_loaded{p}") for p in range(HEADS_RING)]
        s_ready = sem(ctx, "s_ready")
        p_ready = sem(ctx, "p_ready")
        pv_done = sem(ctx, "pv_done")
        m_scored = sem(ctx, "m_scored")
        m_taken = sem(ctx, "m_taken")
        m_neg_ready = sem(ctx, "m_neg_ready")
        m_rows_ready = sem(ctx, "m_rows_ready")
        m_placed = sem(ctx, "m_placed")
        hi_ready = sem(ctx, "hi_ready")
        lo_ready = sem(ctx, "lo_ready")
        o_copied = sem(ctx, "o_copied")
        o_added = sem(ctx, "o_added")
        ctx_stored = [sem(ctx, f"ctx_stored{p}") for p in range(2)]
        v_ones = sem(ctx, "v_ones")
        v_high_ready = sem(ctx, "v_high_ready")
        v_ready = sem(ctx, "v_ready")
        counts_taken = sem(ctx, "counts_taken")
        hot_ready = sem(ctx, "hot_ready")
        counted = sem(ctx, "counted")
        gap_ready = sem(ctx, "gap_ready")
        ratio_ready = sem(ctx, "ratio_ready")
        ids_loaded = sem(ctx, "ids_loaded")
        slots_ready = sem(ctx, "slots_ready")
        listed = sem(ctx, "listed")
        dve_step = sem(ctx, "dve_step2")
        ST_DMAS = 7
        QCS = S // CH
        block = ctx.enter_context(nc.Block())

        def transposed(d, n):
            return d[bass.ds(n // H, 1), bass.ds((n % H) * HD, HD), :].rearrange("a r n -> (a r) n")

        @block.sync
        def _(sp):
            sp.dma_start(pairs[:, :, :, :].rearrange("p a k c -> p (a k c)"), t["token_pairs"]).then_inc(ids_loaded, 16)
            sp.wait_ge(st_ones, 2)

            def load(n, r):
                k_hi, k_lo = transposed(t["k_hi_d"], n), transposed(t["k_lo_d"], n)
                q_hi, q_lo = transposed(t["q_hi_d"], n), transposed(t["q_lo_d"], n)
                bias = t["bias_d"][bass.ds(n % H, 1), :, :].rearrange("a r n -> (a r) n")
                for dst, at, src in ((k_st, 0, k_hi), (q_st, 0, q_hi), (k_st, 32, k_hi), (q_st, 32, q_lo),
                                     (k_st, 64, k_lo), (q_st, 64, q_hi)):
                    sp.dma_start(dst[at:at + HD, r, :].bitcast(F32), src).then_inc(st_loaded[r], 16)
                sp.dma_start(k_st[ROW_BIAS:ROW_BIAS + 2, r, :].bitcast(F32), bias).then_inc(st_loaded[r], 16)

            def place_maxima(n, r):
                sp.wait_ge(m_rows_ready, n + 1)
                for part in range(2):
                    dst = q_st[ROW_MAX + part:ROW_MAX + part + 1, r, :].bitcast(F32).rearrange("o (a b) -> o a b", a=QT)
                    sp.dma_start(dst, m_rows[:, part, :].bitcast(F32)).then_inc(m_placed, 16)

            def store_context(n, qc):
                sp.wait_ge(o_added, 2 + QCS * n + qc + 1)
                at = slice(qc * CH, (qc + 1) * CH)
                sp.dma_start(t["ctx_d"][bass.ds(n * HD, HD), at], high_sums[0:HD, qc % 2, :]).then_inc(ctx_stored[qc % 2], 16)
                sp.dma_start(t["weight_sums_d"][bass.ds(n, 1), at], high_sums[HD:HD + 1, qc % 2, :]).then_inc(ctx_stored[qc % 2], 16)

            load(0, 0)
            load(1, 1)
            place_maxima(0, 0)

            def step_n(n, r, load_ahead=True, maxima=True):
                if load_ahead:
                    sp.wait_ge(pv_done, P_RING + NS * n)
                    load(n + 2, (r + 2) % HEADS_RING)
                for kind, u in ATTEND:
                    if kind == "O":
                        store_context(n, u)
                    if maxima and kind == "W":
                        place_maxima(n + 1, (r + 1) % HEADS_RING)

            with nc.sync.Fori(0, NH // HEADS_RING) as i:
                for r in range(HEADS_RING):
                    step_n(HEADS_RING * i + r, r)
            step_n(NH - 2, (NH - 2) % HEADS_RING, load_ahead=False)
            step_n(NH - 1, (NH - 1) % HEADS_RING, load_ahead=False, maxima=False)
            for p in range(2):
                sp.wait_ge(ctx_stored[p], 32 + 32 * NH * QCS // 2)
            for r in range(HEADS_RING):
                sp.wait_ge(st_loaded[r], 16 * ST_DMAS * len(range(r, NH, HEADS_RING)))
            sp.wait_ge(m_placed, 32 * NH)
            sp.wait_ge(ids_loaded, 16)

        @block.gpsimd
        def _(pool):
            nc.gpsimd.memset(k_st[ROW_BIAS:P, :, :].bitcast(F32), 1.0).then_inc(st_ones, 1)
            nc.gpsimd.memset(q_st[ROW_BIAS:P, :, :].bitcast(F32), 1.0).then_inc(st_ones, 1)
            pool.wait_ge(st_ones, 2)
            nc.gpsimd.memset(v_split[:, :, :, HD:2 * HD].bitcast(F32), 1.0)
            nc.gpsimd.memset(v_whole[:, :, :, HD:2 * HD], 1.0).then_inc(v_ones, 1)
            by_tile = values[:, :].rearrange("p (t h w) -> p t h w", t=TT, h=H)

            def stack_values(n, r):
                src = by_tile[:, bass.ds((n // H) * QT, QT), bass.ds(n % H, 1), :].rearrange("p t a w -> p t (a w)")
                nc.gpsimd.tensor_copy(v_whole[:, r, :, 0:HD], src)
                nc.gpsimd.tensor_copy(v_split[:, r, :, 0:HD], src).then_inc(v_high_ready, 1)
                pool.wait_ge(v_high_ready, n + 1)
                nc.gpsimd.tensor_tensor(v_split[:, r, :, 2 * HD:VS], v_whole[:, r, :, 0:HD], v_split[:, r, :, 0:HD].bitcast(F32),
                                        ALU.subtract).then_inc(v_ready, 1)

            stack_values(0, 0)
            stack_values(1, 1)

            def list_tokens(tiles):
                for a in tiles:
                    for k in range(TOP_K):
                        nc.gpsimd.indirect_dma_start(
                            out=t["list_d"], out_offset=bass.IndirectOffsetOnAxis(ap=t["slot"][:, a, k:k + 1], axis=0),
                            in_=pairs[:, a, k, :], in_offset=None).then_inc(listed, 16)

            def add_sums(n, qc):
                pool.wait_ge(o_copied, 2 + QCS * n + qc + 1)
                high = high_sums[0:HD, qc % 2, :]
                nc.gpsimd.tensor_tensor(high, high, low_sums[:, qc % 2, :], ALU.add).then_inc(o_added, 1)

            def step_n(n, r, list_from=None):
                if list_from is None:
                    pool.wait_ge(pv_done, P_RING + NS * n)
                    stack_values(n + 2, (r + 2) % HEADS_RING)
                for kind, u in ATTEND:
                    if kind == "O":
                        add_sums(n, u)
                        if list_from is not None:
                            first = list_from + u * TT // (2 * QCS)
                            list_tokens(range(first, first + TT // (2 * QCS)))

            with nc.gpsimd.Fori(0, NH // HEADS_RING) as i:
                for r in range(HEADS_RING):
                    step_n(HEADS_RING * i + r, r)
            pool.wait_ge(slots_ready, 1)
            step_n(NH - 2, (NH - 2) % HEADS_RING, list_from=0)
            step_n(NH - 1, (NH - 1) % HEADS_RING, list_from=TT // 2)
            pool.wait_ge(listed, 16 * TT * TOP_K)

        @block.scalar
        def _(act):
            act.sem_inc(p_ready, 2)
            for p in range(2):
                act.sem_inc(ctx_stored[p], 32)
            act.sem_inc(o_copied, 2)
            act.sem_inc(o_added, 2)
            act.wait_ge(gap_ready, 1)
            nc.scalar.activation(ratio[:, :], gap[:, :], ACT.Exp).then_inc(ratio_ready, 1)

            def weights(n, u):
                w = s_span(u)[1]
                act.wait_ge(s_ready, NS * n + u + 1)
                act.wait_ge(pv_done, NS * n + u + 1)
                scores = s_ps[:, u % 2, CH - w:CH]
                if SPLIT[u]:
                    nc.scalar.activation(probs_hi[:, u % P_RING, 0:w], scores, ACT.Exp, scale=SCALE).then_inc(hi_ready, 1)
                nc.scalar.activation(probs[:, u % P_RING, 0:w], scores, ACT.Exp, scale=SCALE).then_inc(p_ready, 1)

            def take_sums(n, qc):
                act.wait_ge(pv_done, P_RING + NS * n + LAST_UNIT[qc] + 1)
                act.wait_ge(ctx_stored[qc % 2], 32 * (QCS // 2 * n + qc // 2 + 1))
                nc.scalar.activation(high_sums[:, qc % 2, :], o_ps[0:2 * HD, qc % 2, :], ACT.Copy)
                act.wait_ge(o_added, QCS * n + qc + 1)
                nc.scalar.activation(low_sums[:, qc % 2, :], o_ps[2 * HD:VS, qc % 2, :], ACT.Copy).then_inc(o_copied, 1)

            with nc.scalar.Fori(0, NH) as n:
                for kind, u in ATTEND:
                    if kind == "S":
                        weights(n, u)
                    if kind == "O":
                        take_sums(n, u)

        @block.vector
        def _(dve):
            step = Links(dve, dve_step)
            V = nc.vector

            def take_maximum(n, m):
                qt, half = M_UNITS[m]
                w = m_span(m)[1]
                dve.wait_ge(m_scored, M_SLOTS * n + m + 1)
                col = qt if half == 0 else QT // 2 + qt
                V.tensor_reduce(m_part[:, col:col + 1], m_ps[:, m % 2, 0:w], AX.X, ALU.max).then_inc(m_taken, 1)

            def fold_maxima(n):
                dve.wait_ge(m_taken, NM * (n + 1))
                step(V.tensor_tensor(m_part[:, QT // 2:QT], m_part[:, QT // 2:QT], m_part[:, QT:QT + QT // 2], ALU.max))
                V.tensor_scalar(m_neg[:, :], m_part[:, 0:QT], -1.0, None, ALU.mult).then_inc(m_neg_ready, 1)

            def maxima_rows(n, placed_before):
                dve.wait_ge(m_scored, M_SLOTS * n + NM + 1)
                if placed_before:
                    dve.wait_ge(m_placed, 32 * n)
                src = m_ps[0:QT, NM % 2, 0:P]
                step(V.tensor_copy(m_rows[:, 0], src))
                V.tensor_tensor(m_rows[:, 1], src, m_rows[:, 0].bitcast(F32), ALU.subtract).then_inc(m_rows_ready, 1)

            def low_part(n, u):
                w = s_span(u)[1]
                dve.wait_ge(p_ready, 2 + NS * n + u + 1)
                V.tensor_tensor(probs_lo[:, u % P_RING, 0:w], probs[:, u % P_RING, 0:w],
                                probs_hi[:, u % P_RING, 0:w].bitcast(F32), ALU.subtract).then_inc(lo_ready, 1)

            def place_tokens():
                numbers, firsts = t["rows_c"][:, 0:E], t["rows_c"][0:1, E:]
                top_val = t["top_val"]
                share = pairs[:, :, :, 1].bitcast(F32)
                V.tensor_tensor(gap[:, :], top_val[:, :, 1], top_val[:, :, 0], ALU.subtract).then_inc(gap_ready, 1)
                step(V.tensor_copy(idx_f[:, :, :], t["top_idx"][:, :, 0:TOP_K]))
                for k in range(TOP_K):
                    last = V.tensor_tensor(hot[:, k], idx_f[:, :, k:k + 1].to_broadcast([P, TT, E]),
                                           numbers.unsqueeze(1).to_broadcast([P, TT, E]), ALU.is_equal)
                step(last)
                V.tensor_tensor(both[:, :, :], hot[:, 0], hot[:, 1], ALU.add).then_inc(hot_ready, 1)
                dve.wait_ge(ratio_ready, 1)
                dve.wait_ge(ids_loaded, 16)
                step(V.tensor_scalar(denom[:, :], ratio[:, :], 1.0, None, ALU.add))
                step(V.reciprocal(denom[:, :], denom[:, :]))
                step(V.tensor_scalar(share[:, :, 0], denom[:, :], MOE_SCALE, None, ALU.mult))
                step(V.tensor_tensor(share[:, :, 1], share[:, :, 0], ratio[:, :], ALU.mult))
                dve.wait_ge(counted, 1)
                step(V.tensor_copy(counts[:, :, :, :], o_ps[:, 1, :].rearrange("p (a t e) -> p a t e", a=2, t=TT)))
                dve.sem_inc(counts_taken, 1)
                for e in range(E):
                    last = V.tensor_tensor_scan(so_far[:, :, e], t["ones"][:, 0:TT], counts[:, 1, :, e], 0.0,
                                                ALU.mult, ALU.add)
                step(last)
                step(V.tensor_scalar(padded_i[:, :], so_far[:, TT - 1, :], float(P - 1), None, ALU.add))
                shift = P.bit_length() - 1
                step(V.tensor_scalar(padded_i[:, :], padded_i[:, :], shift, shift, ALU.logical_shift_right,
                                     ALU.logical_shift_left))
                step(V.tensor_copy(padded[:, :], padded_i[:, :]))
                step(V.tensor_tensor_scan(ends[:, :], t["ones"][:, 0:E], padded[:, :], 0.0, ALU.mult, ALU.add))
                step(V.tensor_tensor(starts[:, :], ends[:, :], padded[:, :], ALU.subtract))
                step(V.tensor_tensor(base[:, :, :], so_far[:, :, :], counts[:, 1], ALU.subtract))
                step(V.tensor_tensor(base[:, :, :], base[:, :, :], counts[:, 0], ALU.add))
                step(V.tensor_tensor(base[:, :, :], base[:, :, :], starts[:, :].unsqueeze(1).to_broadcast([P, TT, E]), ALU.add))
                for k in range(TOP_K):
                    last = V.tensor_tensor(hot[:, k], hot[:, k], base[:, :, :], ALU.mult)
                step(last)
                for k in range(TOP_K):
                    last = V.tensor_reduce(slot_f[:, :, k], hot[:, k], AX.X, ALU.add)
                step(last)
                V.tensor_copy(t["slot"][:, :, :], slot_f[:, :, :]).then_inc(slots_ready, 1)
                step(V.tensor_tensor(passed[:, :, :], firsts.unsqueeze(2).to_broadcast([1, NMT + 1, E]),
                                     ends[0:1, :].unsqueeze(1).to_broadcast([1, NMT + 1, E]), ALU.is_ge))
                step(V.tensor_reduce(te_f[:, :], passed[:, :, :], AX.X, ALU.add))
                V.tensor_scalar(t["tile_expert"][:, :], te_f[:, :], float(E - 1), None, ALU.min)

            for m in range(NM):
                take_maximum(0, m)
            fold_maxima(0)
            maxima_rows(0, False)
            place_tokens()

            def step_n(n, maxima=True):
                for kind, u in ATTEND:
                    if kind == "L":
                        low_part(n, u)
                    if maxima and kind == "M":
                        take_maximum(n + 1, u)
                    if maxima and kind == "X":
                        fold_maxima(n + 1)
                    if maxima and kind == "W":
                        maxima_rows(n + 1, True)

            start = step.n
            per = 2
            with nc.vector.Fori(0, NH - 1) as n:
                step.base, step.n = start + n * per, 0
                step_n(n)
                assert step.n == per, step.n
            step.base, step.n = start + (NH - 1) * per, 0
            step_n(NH - 1, maxima=False)

        @block.tensor
        def _(pe):
            def maximum_tile(n, r, m, first=False):
                qt, half = M_UNITS[m]
                k0, w = m_span(m)
                if m >= 2:
                    pe.wait_ge(m_taken, NM * n + m - 1)
                elif not first:
                    pe.wait_ge(m_rows_ready, n)
                for c0 in range(0, w, CH):
                    cw = min(CH, w - c0)
                    diagonal = k0 + c0 + cw == (qt + 1) * P
                    last = nc.tensor.matmul(m_ps[:, m % 2, c0:c0 + cw], q_st[0:ROW_MAX, r, qt * P:(qt + 1) * P],
                                            k_st[0:ROW_MAX, r, k0 + c0:k0 + c0 + cw], start=True, stop=not diagonal)
                    if diagonal:
                        last = nc.tensor.matmul(m_ps[:, m % 2, c0 + cw - P:c0 + cw], ident_r, mask_m,
                                                start=False, stop=True)
                last.then_inc(m_scored, 1)

            def transpose_maxima(n):
                pe.wait_ge(m_neg_ready, n + 1)
                nc.tensor.transpose(m_ps[0:QT, NM % 2, 0:P], m_neg[:, :], ident).then_inc(m_scored, 1)

            def score_tile(n, r, u):
                qc, kt = S_UNITS[u]
                q0, w = s_span(u)
                more = max(0, 2 * P - w)
                diagonal = q0 == kt * P
                pe.wait_ge(p_ready, NS * n + u + 1)
                last = nc.tensor.matmul(s_ps[:, u % 2, CH - w - more:CH], k_st[0:ROWS, r, kt * P:(kt + 1) * P],
                                        q_st[0:ROWS, r, q0 - more:q0 + w], start=True, stop=not diagonal)
                if diagonal:
                    last = nc.tensor.matmul(s_ps[:, u % 2, CH - w:CH - w + P], ident_r, mask_s, start=False, stop=True)
                last.then_inc(s_ready, 1)

            def value_products(n, r, u, split_before):
                qc, kt = S_UNITS[u]
                q0, w = s_span(u)
                if kt == 0:
                    pe.wait_ge(o_copied, QCS * n + qc + 1)
                at = slice(q0 - qc * CH, CH)
                place = u % P_RING
                if SPLIT[u]:
                    pe.wait_ge(hi_ready, NSPLIT * n + split_before + 1)
                    nc.tensor.matmul(o_ps[0:VS, qc % 2, at], v_split[:, r, kt, :], probs_hi[:, place, 0:w],
                                     start=(kt == 0), stop=True, skip_group_check=True)
                    pe.wait_ge(lo_ready, NSPLIT * n + split_before + 1)
                    last = nc.tensor.matmul(o_ps[0:VS, qc % 2, at], v_split[:, r, kt, :], probs_lo[:, place, 0:w],
                                            start=False, stop=True, skip_group_check=True)
                else:
                    pe.wait_ge(p_ready, 2 + NS * n + u + 1)
                    last = nc.tensor.matmul(o_ps[0:2 * HD, qc % 2, at], v_whole[:, r, kt, :], probs[:, place, 0:w],
                                            start=False, stop=True, skip_group_check=True)
                last.then_inc(pv_done, 1)

            pe.sem_inc(pv_done, P_RING)
            pe.wait_ge(st_loaded[0], 16 * ST_DMAS)
            for m in range(NM):
                maximum_tile(0, 0, m, first=True)
            transpose_maxima(0)
            pe.wait_ge(hot_ready, 1)
            hot2 = both[:, :, :].rearrange("p t e -> p (t e)")
            nc.tensor.matmul(o_ps[:, 1, 0:TT * E], t["triu"], hot2, start=True, stop=True)
            nc.tensor.matmul(o_ps[:, 1, TT * E:2 * TT * E], t["ones"], hot2, start=True, stop=True).then_inc(counted, 1)
            pe.wait_ge(counts_taken, 1)
            pe.wait_ge(v_ones, 1)

            def step_n(n, r, st_round, maxima=True):
                r1 = (r + 1) % HEADS_RING
                pe.wait_ge(m_placed, 32 * (n + 1))
                pe.wait_ge(v_ready, n + 1)
                if maxima:
                    pe.wait_ge(st_loaded[r1], 16 * ST_DMAS * st_round)
                for kind, u in ATTEND:
                    if kind == "S":
                        score_tile(n, r, u)
                    if kind == "V":
                        value_products(n, r, u, sum(SPLIT[:u]))
                    if maxima and kind == "M":
                        maximum_tile(n + 1, r1, u)
                    if maxima and kind == "W":
                        transpose_maxima(n + 1)

            with nc.tensor.Fori(0, NH // HEADS_RING) as i:
                for r in range(HEADS_RING):
                    step_n(HEADS_RING * i + r, r, i + 1 + (r + 1) // HEADS_RING)
            n = NH - 2
            step_n(n, n % HEADS_RING, (n + 1) // HEADS_RING + 1)
            step_n(NH - 1, (NH - 1) % HEADS_RING, 0, maxima=False)





def output(nc, sb, ps, sem, t):
    UW = 2 * P
    TPU = UW // P
    NU = T // UW
    X_RING = 4
    KH = KD // 2
    assert NU == 2 * E
    w_hi, w_lo = t["w_hi"], t["w_lo"]
    with ExitStack() as ctx:
        wo_hi = sb(ctx, "wo_hi", [P, G, D], F32R)
        wo_lo = sb(ctx, "wo_lo", [P, G, D], F32R)
        bo_row = sb(ctx, "bo_row", [P, D], F32)
        spread = sb(ctx, "spread", [2 * H, D], F32R)
        inv_st = sb(ctx, "inv_st", [2 * H, 2, UW], F32R)
        sums = sb(ctx, "sums", [P, 2, G, UW], F32)
        ctx_hi = sb(ctx, "ctx_hi", [P, 2, G, UW], F32R)
        ctx_lo = sb(ctx, "ctx_lo", [P, 2, G, UW], F32R)
        xb = sb(ctx, "xb", [P, X_RING, TPU, D], F32)
        w_raw = sb(ctx, "gu_raw", [P, 2, KH, 2 * F], F32)
        wo_raw = xb[:, 2:4].rearrange("p r j n -> p (r j) n")
        inv, spread_raw = xb[:, 1, 0, :], xb[0:2 * H, 1, 1, :]
        inv_hi, inv_lo = (c[:, 1].rearrange("p g n -> p (g n)")[:, 0:NH * S // P] for c in (ctx_hi, ctx_lo))
        inv_ps = ps(ctx, "inv_ps", [P, 2, G, UW])
        out_ps = ps(ctx, "out_ps", [P, 2, TPU, D])

        small_loaded = sem(ctx, "o_small_loaded")
        wo_loaded = sem(ctx, "wo_loaded")
        wo_hi_ready = sem(ctx, "wo_hi_ready")
        wo_ready = sem(ctx, "wo_ready")
        weight_sums_loaded = sem(ctx, "weight_sums_loaded")
        inverted = sem(ctx, "inverted")
        inv_hi_ready = sem(ctx, "inv_hi_ready")
        inv_ready = sem(ctx, "inv_ready")
        inv_stored = sem(ctx, "inv_stored")
        inv_loaded = [sem(ctx, f"inv_loaded{p}") for p in range(2)]
        sums_loaded = [sem(ctx, f"sums_loaded{p}") for p in range(2)]
        x_loaded = [sem(ctx, f"ox_loaded{p}") for p in range(X_RING)]
        w_loaded = [sem(ctx, f"w_loaded{p}") for p in range(2)]
        w_hi_ready = sem(ctx, "gu_hi_ready")
        w_lo_ready = sem(ctx, "gu_lo_ready")
        spread_ready = sem(ctx, "spread_ready")
        inv_spread = sem(ctx, "inv_spread")
        ctx_ready = sem(ctx, "ctx_ready")
        hi_ready = sem(ctx, "ctx_hi_ready")
        lo_ready = sem(ctx, "ctx_lo_ready")
        xb_ready = sem(ctx, "xb_ready")
        projected = sem(ctx, "projected")
        taken = sem(ctx, "taken")
        stored = [sem(ctx, f"stored{p}") for p in range(X_RING)]
        block = ctx.enter_context(nc.Block())

        @block.sync
        def _(sp):
            rows_of = lambda d: d.rearrange("n (a b) -> (n a) b", b=NH * S // P)

            def columns(u):
                return u // (NU // B), bass.ds((u % (NU // B)) * UW, UW)

            def load_sums(u, par):
                b, at = columns(u)
                sp.dma_start(sums[:, par], t["ctx_d"][bass.ds(b * D, D), at].rearrange("(g p) n -> p g n", p=P)).then_inc(sums_loaded[par], 16)

            def load_inverses(u, par):
                b, at = columns(u)
                for part in range(2):
                    sp.dma_start(inv_st[part * H:(part + 1) * H, par, :].bitcast(F32),
                                 t["inverse_d"][part, bass.ds(b * H, H), at]).then_inc(inv_loaded[par], 16)

            def x_rows(d, u):
                return d[bass.ds(u * UW, UW), :].rearrange("(j p) d -> p j d", p=P)

            def load_x(u, r):
                sp.dma_start(xb[:, r], x_rows(t["x"], u)).then_inc(x_loaded[r], 16)

            def load_weights(e, half):
                for part, name in enumerate(("gate_w", "up_w")):
                    src = t[name][bass.ds(e, 1), half * KH * P:(half + 1) * KH * P, :]
                    sp.dma_start(w_raw[:, half, :, part * F:(part + 1) * F],
                                 src.rearrange("a (k p) f -> p (a k) f", p=P)).then_inc(w_loaded[half], 16)

            sp.dma_start(inv, rows_of(t["weight_sums_d"])).then_inc(weight_sums_loaded, 16)
            sp.dma_start(wo_raw, t["Wo"].rearrange("(g p) n -> p g n", p=P)).then_inc(wo_loaded, 16)
            sp.dma_start(spread_raw, t["spread"]).then_inc(small_loaded, 16)
            sp.dma_start(bo_row[:, :], t["bo"].partition_broadcast(P)).then_inc(small_loaded, 16)
            for u in range(2):
                load_sums(u, u)
            sp.wait_ge(inv_ready, 1)
            for part, src in enumerate((inv_hi, inv_lo)):
                sp.dma_start(rows_of(t["inverse_d"][part]), src.bitcast(F32)).then_inc(inv_stored, 16)
            sp.wait_ge(inv_stored, 32)
            for u in range(2):
                load_inverses(u, u)
            load_x(0, 0)
            for half in range(2):
                load_weights(0, half)
            sp.wait_ge(spread_ready, 1)
            load_x(1, 1)
            sp.wait_ge(wo_ready, 1)
            load_x(2, 2)

            def unit(u, e, r, sums_ahead=True, x_ahead=True):
                if sums_ahead:
                    sp.wait_ge(inv_spread, u + 1)
                    load_inverses(u + 2, r % 2)
                    sp.wait_ge(lo_ready, u + 1)
                    load_sums(u + 2, r % 2)
                    sp.wait_ge(w_lo_ready, u + 1)
                    load_weights(e + 1, r % 2)
                sp.wait_ge(taken, 2 * TPU + TPU * (u + 1))
                sp.dma_start(x_rows(t["out"], u), xb[:, r]).then_inc(stored[r], 16)
                if x_ahead:
                    ahead = (r + X_RING - 1) % X_RING
                    sp.wait_ge(stored[ahead], 16 * ((u + X_RING - 1) // X_RING + 1))
                    load_x(u + X_RING - 1, ahead)

            with nc.sync.Fori(0, NU // X_RING - 1) as i:
                for r in range(X_RING):
                    unit(X_RING * i + r, X_RING // 2 * i + r // 2, r)
            for u in range(NU - X_RING, NU):
                unit(u, u // 2, u % X_RING, sums_ahead=u < NU - 2, x_ahead=u == NU - X_RING)
            for p in range(X_RING):
                sp.wait_ge(stored[p], 16 * (NU // X_RING) + 16)

        @block.gpsimd
        def _(pool):
            pool.wait_ge(small_loaded, 32)

            def add_bias(u, r):
                pool.wait_ge(x_loaded[r], 16 * (u // X_RING + 1))
                for j in range(TPU):
                    nc.gpsimd.tensor_tensor(xb[:, r, j], xb[:, r, j], bo_row[:, :], ALU.add).then_inc(xb_ready, 1)

            def place(w, e, r):
                half = r % 2
                return w[:, bass.ds(e, 1), half * KH:(half + 1) * KH, :].rearrange("p a k f -> p (a k) f")

            with nc.gpsimd.Fori(0, NU // X_RING) as i:
                for r in range(X_RING):
                    u, e = X_RING * i + r, X_RING // 2 * i + r // 2
                    pool.wait_ge(w_hi_ready, u + 1)
                    add_bias(u, r)
                    nc.gpsimd.tensor_tensor(place(w_lo, e, r), w_raw[:, r % 2], place(w_hi, e, r).bitcast(F32),
                                            ALU.subtract).then_inc(w_lo_ready, 1)

        @block.scalar
        def _(act):
            act.sem_inc(projected, 2)
            for p in range(X_RING):
                act.sem_inc(stored[p], 16)
            act.wait_ge(wo_loaded, 16)
            nc.scalar.activation(wo_hi[:, :, :], wo_raw, ACT.Copy).then_inc(wo_hi_ready, 1)

            def high(u, r):
                act.wait_ge(ctx_ready, u + 1)
                act.wait_ge(projected, u + 1)
                nc.scalar.activation(ctx_hi[:, r % 2], sums[:, r % 2], ACT.Copy).then_inc(hi_ready, 1)

            with nc.scalar.Fori(0, NU // X_RING) as i:
                for r in range(X_RING):
                    u, e, half = X_RING * i + r, X_RING // 2 * i + r // 2, r % 2
                    act.wait_ge(w_loaded[half], 32 * (u // 2 + 1))
                    high(u, r)
                    dst = w_hi[:, bass.ds(e, 1), half * KH:(half + 1) * KH, :].rearrange("p a k f -> p (a k) f")
                    nc.scalar.activation(dst, w_raw[:, half], ACT.Copy).then_inc(w_hi_ready, 1)

        @block.vector
        def _(dve):
            V = nc.vector
            dve.sem_inc(taken, 2 * TPU)
            dve.wait_ge(weight_sums_loaded, 16)
            V.reciprocal(inv, inv).then_inc(inverted, 1)
            dve.wait_ge(inverted, 1)
            V.tensor_copy(inv_hi, inv).then_inc(inv_hi_ready, 1)
            dve.wait_ge(inv_hi_ready, 1)
            V.tensor_tensor(inv_lo, inv, inv_hi.bitcast(F32), ALU.subtract).then_inc(inv_ready, 1)
            dve.wait_ge(small_loaded, 32)
            V.tensor_copy(spread[:, :], spread_raw).then_inc(spread_ready, 1)
            dve.wait_ge(wo_hi_ready, 1)
            V.tensor_tensor(wo_lo[:, :, :], wo_raw, wo_hi[:, :, :].bitcast(F32), ALU.subtract).then_inc(wo_ready, 1)

            def context(u, r):
                dve.wait_ge(sums_loaded[r % 2], 16 * (u // 2 + 1))
                dve.wait_ge(inv_spread, u + 1)
                V.tensor_tensor(sums[:, r % 2], sums[:, r % 2], inv_ps[:, r % 2], ALU.mult).then_inc(ctx_ready, 1)
                dve.wait_ge(hi_ready, u + 1)
                V.tensor_tensor(ctx_lo[:, r % 2], sums[:, r % 2], ctx_hi[:, r % 2].bitcast(F32), ALU.subtract).then_inc(lo_ready, 1)

            def take(u, r):
                dve.wait_ge(projected, 2 + u + 1)
                dve.wait_ge(xb_ready, TPU * (u + 1))
                for j in range(TPU):
                    V.tensor_tensor(xb[:, r, j], out_ps[:, r % 2, j], xb[:, r, j], ALU.add).then_inc(taken, 1)

            def unit(u, r, ahead=True):
                if ahead:
                    context(u + 1, r + 1)
                take(u, r)

            context(0, 0)
            with nc.vector.Fori(0, NU // X_RING - 1) as i:
                for r in range(X_RING):
                    unit(X_RING * i + r, r)
            for r in range(X_RING):
                unit(NU - X_RING + r, r, ahead=r < X_RING - 1)

        @block.tensor
        def _(pe):
            def spread_inverses(u, r, first=False):
                pe.wait_ge(inv_loaded[r % 2], 32 * (u // 2 + 1))
                if not first:
                    pe.wait_ge(ctx_ready, u - 1)
                for g in range(G):
                    last = nc.tensor.matmul(inv_ps[:, r % 2, g], spread[:, g * P:(g + 1) * P], inv_st[:, r % 2, :],
                                            start=True, stop=True)
                last.then_inc(inv_spread, 1)

            def project_unit(u, r):
                pe.wait_ge(lo_ready, u + 1)
                pe.wait_ge(taken, TPU * (u + 1))
                for j in range(TPU):
                    rows = slice(j * P, (j + 1) * P)
                    for g in range(G):
                        for n, (lhs, w) in enumerate(((ctx_hi, wo_hi), (ctx_hi, wo_lo), (ctx_lo, wo_hi))):
                            last = nc.tensor.matmul(out_ps[:, r % 2, j], lhs[:, r % 2, g, rows], w[:, g, :],
                                                    start=(g == 0 and n == 0), stop=(g == G - 1 and n == 2))
                last.then_inc(projected, 1)

            pe.wait_ge(spread_ready, 1)
            for u in range(2):
                spread_inverses(u, u, first=True)
            pe.wait_ge(wo_ready, 1)
            with nc.tensor.Fori(0, NU // X_RING - 1) as i:
                for r in range(X_RING):
                    project_unit(X_RING * i + r, r)
                    spread_inverses(X_RING * i + r + 2, r)
            for r in range(X_RING):
                project_unit(NU - X_RING + r, r)
                if r < X_RING - 2:
                    spread_inverses(NU - X_RING + r + 2, r)


def experts(nc, sb, ps, sem, t):
    ident, tile_expert = t["ident"], t["tile_expert"]
    w_hi, w_lo, out = t["w_hi"], t["w_lo"], t["out"]
    with ExitStack() as ctx:
        w_down = sb(ctx, "w_down", [P, E, KF, D], F32)
        lists = sb(ctx, "lists", [P, NMT, 2], I32)
        row_in = sb(ctx, "row_in", [P, 2], I32)
        row_out = sb(ctx, "row_out", [P, 2], I32)
        share = sb(ctx, "share", [P, 2], F32)
        xg = sb(ctx, "xg", [P, 2, D], F32)
        x_hi = sb(ctx, "ex_hi", [P, 2, KD, P], F32R)
        x_lo = sb(ctx, "ex_lo", [P, 2, KD, P], F32R)
        th = sb(ctx, "th", [P, 2, F], F32)
        gated = sb(ctx, "gated", [P, 2, F], F32)
        inner = sb(ctx, "inner", [P, 2, F], F32)
        inner_t = sb(ctx, "inner_t", [P, 2, KF, P], F32)
        y = sb(ctx, "y", [P, 2, D], F32)
        xt_ps = ps(ctx, "xt_ps", [P, 2, KD, P])
        h_ps = ps(ctx, "h_ps", [P, 2, 2 * F])
        it_ps = ps(ctx, "it_ps", [P, 2, CH])
        y_ps = ps(ctx, "y_ps", [P, 2, D])

        lists_loaded = sem(ctx, "lists_loaded")
        w_down_loaded = sem(ctx, "w_down_loaded")
        held = sem(ctx, "held")
        row_in_ready = sem(ctx, "row_in_ready")
        share_ready = sem(ctx, "share_ready")
        xg_loaded = [sem(ctx, f"xg_loaded{p}") for p in range(2)]
        x_turned = sem(ctx, "x_turned")
        x_hi_ready = sem(ctx, "ex_hi_ready")
        x_lo_ready = sem(ctx, "ex_lo_ready")
        h_ready = sem(ctx, "h_ready")
        th_ready = sem(ctx, "th_ready")
        gated_ready = sem(ctx, "gated_ready")
        inner_ready = sem(ctx, "inner_ready")
        inner_turned = sem(ctx, "inner_turned")
        inner_t_ready = sem(ctx, "inner_t_ready")
        y_made = sem(ctx, "y_made")
        y_scaled = sem(ctx, "y_scaled")
        added = sem(ctx, "added")
        block = ctx.enter_context(nc.Block())

        def over_tiles(engine, step):
            loops = (NMT - 3) // 2
            with engine.Fori(0, loops) as i:
                for p in range(2):
                    step(2 * i + p, p, NMT)
            for tile in range(2 * loops, NMT):
                step(tile, tile % 2, NMT - tile)

        @block.sync
        def _(sp):
            sp.dma_start(lists[:, :, :], t["list_d"].rearrange("(n p) c -> p n c", p=P)).then_inc(lists_loaded, 16)
            for e in range(E):
                sp.dma_start(w_down[:, e], t["down_w"][e].rearrange("(k p) n -> p k n", p=P)).then_inc(w_down_loaded, 16)

        @block.gpsimd
        def _(pool):
            def hold():
                pool.sem_inc(held, 1)

            def fetch(n, p):
                pool.wait_ge(x_turned, n + 1)
                hold()
                nc.gpsimd.tensor_copy(row_in[:, p:p + 1], lists[:, bass.ds(n, 1), 0]).then_inc(row_in_ready, 1)
                pool.wait_ge(row_in_ready, n + 1)
                hold()
                nc.gpsimd.indirect_dma_start(out=xg[:, p, :], out_offset=None, in_=t["xn_d"],
                                             in_offset=bass.IndirectOffsetOnAxis(ap=row_in[:, p:p + 1], axis=0)
                                             ).then_inc(xg_loaded[p], 16)

            def take_shares(n, p):
                nc.gpsimd.tensor_copy(row_out[:, p:p + 1], lists[:, bass.ds(n, 1), 0])
                nc.gpsimd.tensor_copy(share[:, p:p + 1], lists[:, bass.ds(n, 1), 1].bitcast(F32)).then_inc(share_ready, 1)

            def add_rows(n, p):
                pool.wait_ge(share_ready, n + 1)
                pool.wait_ge(y_scaled, 2 + n + 1)
                hold()
                nc.gpsimd.indirect_dma_start(out=out, out_offset=bass.IndirectOffsetOnAxis(ap=row_out[:, p:p + 1], axis=0),
                                             in_=y[:, p, :], in_offset=None, compute_op=ALU.add).then_inc(added, 16)

            pool.sem_inc(x_turned, 2)
            pool.wait_ge(lists_loaded, 16)
            take_shares(0, 0)
            for n in range(4):
                fetch(n, n % 2)

            def step(n, p, left):
                if left > 4:
                    fetch(n + 4, p)
                add_rows(n, p)
                if left > 1:
                    take_shares(n + 1, 1 - p)
                pool.wait_ge(added, 16 * (n + 1))

            loops = (NMT - 4) // 2
            with nc.gpsimd.Fori(0, loops) as i:
                for p in range(2):
                    step(2 * i + p, p, NMT)
            for n in range(2 * loops, NMT):
                step(n, n % 2, NMT - n)

        @block.scalar
        def _(act):
            def high(n, p):
                act.wait_ge(x_turned, 2 + n + 1)
                act.wait_ge(h_ready, n + 1)
                nc.scalar.activation(x_hi[:, p], xt_ps[:, p], ACT.Copy).then_inc(x_hi_ready, 1)

            def half_tanh(n, p):
                act.wait_ge(h_ready, 2 + n + 1)
                act.wait_ge(inner_ready, n + 1)
                nc.scalar.activation(th[:, p], h_ps[:, p, 0:F], ACT.Tanh, scale=0.5).then_inc(th_ready, 1)

            def scale(n, p):
                act.wait_ge(y_made, 2 + n + 1)
                act.wait_ge(share_ready, n + 1)
                nc.scalar.activation(y[:, p], y_ps[:, p], ACT.Copy, scale=share[:, p:p + 1]).then_inc(y_scaled, 1)

            act.sem_inc(y_scaled, 2)
            high(0, 0)
            high(1, 1)
            half_tanh(0, 0)

            def step(n, p, left):
                if left > 1:
                    half_tanh(n + 1, 1 - p)
                if left > 2:
                    high(n + 2, p)
                scale(n, p)

            over_tiles(nc.scalar, step)

        @block.vector
        def _(dve):
            V = nc.vector

            def low(n, p):
                dve.wait_ge(x_hi_ready, n + 1)
                V.tensor_tensor(x_lo[:, p], xt_ps[:, p], x_hi[:, p].bitcast(F32), ALU.subtract).then_inc(x_lo_ready, 1)

            def gate(n, p):
                dve.wait_ge(th_ready, n + 1)
                V.scalar_tensor_tensor(gated[:, p], th[:, p], 1.0, h_ps[:, p, 0:F], ALU.add, ALU.mult).then_inc(gated_ready, 1)
                dve.wait_ge(gated_ready, n + 1)
                dve.wait_ge(inner_turned, n + 1)
                V.scalar_tensor_tensor(inner[:, p], gated[:, p], 0.5, h_ps[:, p, F:2 * F], ALU.mult, ALU.mult).then_inc(inner_ready, 1)

            def take_turned(n, p):
                dve.wait_ge(inner_turned, 2 + n + 1)
                dve.wait_ge(y_made, n + 1)
                V.tensor_copy(inner_t[:, p], it_ps[:, p, 0:F].rearrange("p (k n) -> p k n", k=KF)).then_inc(inner_t_ready, 1)

            for s in (x_lo_ready, inner_ready, inner_t_ready):
                dve.sem_inc(s, 2)
            low(0, 0)
            low(1, 1)
            gate(0, 0)

            def step(n, p, left):
                take_turned(n, p)
                if left > 1:
                    gate(n + 1, 1 - p)
                if left > 2:
                    low(n + 2, p)

            over_tiles(nc.vector, step)

        @block.tensor
        def _(pe):
            def expert_of(n):
                return pe.value_load(tile_expert[0:1, bass.ds(n, 1)], min_val=0, max_val=E - 1)

            def turn_rows(n, p):
                pe.wait_ge(xg_loaded[p], 16 * (n // 2 + 1))
                pe.wait_ge(x_lo_ready, n + 1)
                for k in range(KD):
                    last = nc.tensor.transpose(xt_ps[:, p, k], xg[:, p, k * P:(k + 1) * P], ident)
                last.then_inc(x_turned, 1)

            def gate_up(n, p):
                e = expert_of(n)
                pe.wait_ge(x_lo_ready, 2 + n + 1)
                pe.wait_ge(inner_ready, n + 1)
                for k in range(KD):
                    for m, (lhs, w) in enumerate(((x_hi, w_hi), (x_hi, w_lo), (x_lo, w_hi))):
                        rhs = w[:, bass.ds(e, 1), k, :].rearrange("p a f -> p (a f)")
                        last = nc.tensor.matmul(h_ps[:, p], lhs[:, p, k], rhs, start=(k == 0 and m == 0),
                                                stop=(k == KD - 1 and m == 2))
                last.then_inc(h_ready, 1)

            def turn_inner(n, p):
                pe.wait_ge(inner_ready, 2 + n + 1)
                pe.wait_ge(inner_t_ready, n + 1)
                for k in range(KF):
                    last = nc.tensor.transpose(it_ps[:, p, k * P:(k + 1) * P], inner[:, p, k * P:(k + 1) * P], ident)
                last.then_inc(inner_turned, 1)

            def down(n, p):
                e = expert_of(n)
                pe.wait_ge(inner_t_ready, 2 + n + 1)
                pe.wait_ge(y_scaled, n + 1)
                for k in range(KF):
                    rhs = w_down[:, bass.ds(e, 1), k, :].rearrange("p a n -> p (a n)")
                    last = nc.tensor.matmul(y_ps[:, p], inner_t[:, p, k], rhs, start=(k == 0), stop=(k == KF - 1))
                last.then_inc(y_made, 1)

            for s in (h_ready, inner_turned, y_made):
                pe.sem_inc(s, 2)
            turn_rows(0, 0)
            turn_rows(1, 1)
            gate_up(0, 0)
            pe.wait_ge(w_down_loaded, 16 * E)

            def step(n, p, left):
                if left > 1:
                    gate_up(n + 1, 1 - p)
                turn_inner(n, p)
                if left > 2:
                    turn_rows(n + 2, p)
                down(n, p)

            over_tiles(nc.tensor, step)


def kernel(**inputs):
    import numpy as np
    import concourse.bacc as bacc
    from concourse.bass_utils import run_bass_kernel_spmd

    pre = {n: np.ascontiguousarray(a) for n, a in inputs.items()}
    i, j = np.arange(P)[:, None], np.arange(P)[None, :]
    f32 = np.float32

    def columns(a):
        return np.ascontiguousarray(a.reshape(KD, P, -1).transpose(1, 0, 2).reshape(P, -1))

    arrays = {
        "x": pre["L0_attn_x"].reshape(T, D),
        "Wq": pre["L0_attn_Wq"], "bq": columns(pre["L0_attn_bq"]), "Wk": pre["L0_attn_Wk"], "bk": columns(pre["L0_attn_bk"]),
        "Wv": pre["L0_attn_Wv"], "bv": pre["L0_attn_bv"], "Wo": pre["L0_attn_Wo"], "bo": pre["L0_attn_bo"],
        "rwT": columns(pre["L0_ffn_router_w"].T), "nw": columns(pre["L0_ffn_norm_w"]),
        "gate_w": pre["L0_ffn_gate_w"], "up_w": pre["L0_ffn_up_w"], "down_w": pre["L0_ffn_down_w"],
        "cst": np.concatenate([i == j, np.where(j <= i, 0.0, NEG), np.where(j >= i, 0.0, NEG), i < j,
                               np.ones((P, P))], axis=1).astype(f32),
        "rows": np.tile(np.concatenate([np.arange(E), P * np.arange(NMT + 1)]).astype(f32), (P, 1)),
        "alibi": ((2.0 ** (-8.0 / H)) ** np.arange(1, H + 1)[:, None] * np.arange(1 - S, 1)[None, :] / SCALE).astype(f32),
        "spread": np.tile(np.arange(H)[:, None] == np.arange(D)[None, :] // HD, (2, 1)).astype(f32),
        "token_pairs": np.stack([np.repeat(i + P * np.arange(TT)[None, :], TOP_K, axis=1),
                                 np.zeros((P, TT * TOP_K))], axis=-1).reshape(P, -1).astype(np.int32),
        "no_pairs": np.stack([T + np.arange(NMT * P) % P, np.zeros(NMT * P)], axis=-1).reshape(P, -1).astype(np.int32),
        "no_rows": np.zeros((P, D), f32),
    }
    nc = bacc.Bacc("TRN2", target_bir_lowering=False, num_devices=1)
    args = {n: nc.dram_tensor(f"in_{n}", a.shape, mybir.dt.from_np(a.dtype), kind="ExternalInput").ap()
            for n, a in arrays.items()}
    args["out"] = nc.dram_tensor("out", (T + P, D), F32, kind="ExternalOutput").ap()
    attention_and_experts(nc, **args)
    r = run_bass_kernel_spmd(nc, [{f"in_{n}": a for n, a in arrays.items()}], core_ids=[0])
    return np.asarray(r.results[0]["out"])[:T].reshape(B, S, D)
```

```python
from contextlib import ExitStack

import concourse.bass as bass
from concourse import mybir

F32 = mybir.dt.float32
F32R = mybir.dt.float32r
BF16 = mybir.dt.bfloat16
I32 = mybir.dt.int32
U32 = mybir.dt.uint32
ACT = mybir.ActivationFunctionType
ALU = mybir.AluOpType
AX = mybir.AxisListType

P = 128
B, S, D, H = 2, 2048, 512, 16
HD = D // H
E, TOP_K = 8, 2
F = 2048 // E
T = B * S
TT = T // P
QT = S // P
KD = D // P
KF = F // P
CH = 512
TPC = CH // P
NCH = T // CH
G = D // P
HPG = P // HD
NH = B * H
NMT = (TOP_K * T + E * (P - 1)) // P
LN_EPS, RMS_EPS = 1e-5, 1e-6
MOE_SCALE = E / TOP_K
SCALE = float(HD) ** -0.5
NEG = -float(2 ** 100)

ROW_BIAS, ROW_MAX, ROWS = 96, 98, 100

S_UNITS = [(qc, kt) for qc in range(S // CH) for kt in range(TPC * (qc + 1))]
NS = len(S_UNITS)
M_WIDE = 512
M_PARTS = S // M_WIDE
M_UNITS = [(qt, part) for qt in range(QT) for part in range((qt * P) // M_WIDE + 1)]
NM = len(M_UNITS)
M_SLOTS = NM + 1


def s_span(u):
    qc, kt = S_UNITS[u]
    q0 = max(CH * qc, P * kt)
    return q0, CH * (qc + 1) - q0


def m_span(m):
    qt, part = M_UNITS[m]
    k0 = part * M_WIDE
    return k0, min((qt + 1) * P, k0 + M_WIDE) - k0


LAST_UNIT = [max(u for u in range(NS) if S_UNITS[u][0] == qc) for qc in range(S // CH)]
SPLIT = [s_span(u)[1] > P for u in range(NS)]
NSPLIT = sum(SPLIT)
ON_POOL = [SPLIT[u] and sum(SPLIT[:u]) % 9 in (1, 3, 5, 7, 8) for u in range(NS)]
NPOOL = sum(ON_POOL)
HIGH_ON_DVE = [SPLIT[u] and sum(SPLIT[:u]) % 6 == 3 for u in range(NS)]
PV_LAG = 6
HIGH_LAG = 1
LOW_LAG = 2


C_AT = (8, 14)
M_END = 0.87


def attend_order():
    total, m_total = sum(s_span(u)[1] for u in range(NS)), sum(m_span(m)[1] for m in range(NM))
    order, m, done, m_done, w_at = [], 0, 0, 0, None
    for u in range(NS):
        order.append(("S", u, 0))
        done += s_span(u)[1]
        for kind, lag, has in (("H", HIGH_LAG, HIGH_ON_DVE), ("L", LOW_LAG, SPLIT)):
            if has[(u - lag) % NS]:
                order.append((kind, (u - lag) % NS, int(u < lag)))
        while m < NM and m_done <= done / (M_END * total) * m_total:
            order.append(("M", m, 0))
            m_done += m_span(m)[1]
            m += 1
            if m == NM:
                order.append(("X", 0, 0))
                w_at = u + 2
        if u == w_at:
            order.append(("W", 0, 0))
        if u in C_AT:
            order.append(("C", C_AT.index(u), 0))
        order.append(("V", (u - PV_LAG) % NS, int(u < PV_LAG)))
        if (u - PV_LAG - 1) % NS in LAST_UNIT:
            order.append(("O", LAST_UNIT.index((u - PV_LAG - 1) % NS), int(u < PV_LAG + 1)))
    return order


ATTEND = attend_order()
HEADS_RING = 3
P_RING = 8
M_BUFS, S_BUFS = 4, 2
LOOPS = (NH - 2) // HEADS_RING
assert LOOPS * HEADS_RING == NH - 2

EDGE_ON_POOL = [ON_POOL[u] and u + PV_LAG >= NS for u in range(NS)]


def low_count(by_pool, h, u, edge):
    edge_pool, split_until = sum(EDGE_ON_POOL), sum(SPLIT[:u]) + 1
    pool_until = sum((EDGE_ON_POOL if edge else ON_POOL)[:u]) + 1
    first = isinstance(h, int) and h == 0
    if by_pool:
        return pool_until if first else NPOOL * h + (edge_pool - NPOOL + pool_until)
    dve_until = split_until - pool_until + 1
    return dve_until if first else (NSPLIT - NPOOL) * h + (NPOOL - edge_pool + dve_until)


VS = 3 * HD
STEPS_PER_PAIR = 34


class Links:

    def __init__(self, eng, sem):
        self.eng, self.sem, self.base, self.n = eng, sem, 0, 0

    def __call__(self, ins):
        self.n += 1
        ins.then_inc(self.sem, 1)
        self.eng.wait_ge(self.sem, self.base + self.n)


def attention_and_experts(nc, x, Wq, bq, Wk, bk, Wv, bv, Wo, bo, rwT, nw, gate_w, up_w, down_w,
                          cst, rows, alibi, spread, token_pairs, no_pairs, no_rows, out):
    with ExitStack() as top:
        def dram(name, shape, dt):
            return nc.dram_tensor(name, shape, dt).ap()

        q_hi_d, q_lo_d = dram("q_hi_d", [B, D, S], F32), dram("q_lo_d", [B, D, S], F32)
        k_hi_d, k_lo_d = dram("k_hi_d", [B, D, S], F32), dram("k_lo_d", [B, D, S], F32)
        ctx_d = dram("ctx_d", [B * D, S], F32)
        weight_sums_d = dram("weight_sums_d", [NH, S], F32)
        inverse_d = dram("inverse_d", [2, NH, S], F32)
        bias_d = dram("bias_d", [H, 2, S], F32)
        xn_d = dram("xn_d", [T + P, D], F32)
        list_d = dram("list_d", [NMT * P, 2], I32)

        def sb(ctx, name, shape, dt):
            return ctx.enter_context(nc.sbuf_tensor(name, shape, dt))

        def ps(ctx, name, shape, dt=F32):
            return ctx.enter_context(nc.psum_tensor(name, shape, dt))

        def sem(ctx, name):
            return ctx.enter_context(nc.semaphore(name))

        consts = sb(top, "consts", [P, 5, P], F32)
        ident, triu, ones = consts[:, 0, :], consts[:, 3, :], consts[:, 4, :]
        mask_r = sb(top, "mask_r", [P, 3, P], BF16)
        ident_r, mask_m, mask_s = mask_r[:, 0, :], mask_r[:, 1, :], mask_r[:, 2, :]
        rows_c = sb(top, "rows_c", [P, E + NMT + 1], F32)
        top_val = sb(top, "top_val", [P, TT, 8], F32)
        top_idx = sb(top, "top_idx", [P, TT, 8], U32)
        slot = sb(top, "slot", [P, TT, TOP_K], U32)
        tile_expert = sb(top, "tile_expert", [1, NMT + 1], I32)

        with ExitStack() as early:
            values = sb(early, "values", [P, TT * D], F32)
            project(nc, sb, ps, sem, locals())
            attend(nc, sb, ps, sem, locals())
        with ExitStack() as late:
            lists = sb(late, "lists", [P, NMT, 2], I32)
            w_hi = sb(late, "gu_hi", [P, E, KD, 2 * F], F32R)
            w_lo = sb(late, "gu_lo", [P, E, KD, 2 * F], F32R)
            output(nc, sb, ps, sem, locals())
            experts(nc, sb, ps, sem, locals())



def project(nc, sb, ps, sem, t):
    x = t["x"]
    consts, mask_r, ident = t["consts"], t["mask_r"], t["ident"]
    values, top_val, top_idx = t["values"], t["top_val"], t["top_idx"]
    NJ = 2 * G + TPC
    BANKS = 4
    QK_RING = 4
    with ExitStack() as ctx:
        w_raw = sb(ctx, "w_raw", [P, KD, D], F32)
        w_hi = sb(ctx, "w_hi", [P, 3, KD, D], F32R)
        w_lo = sb(ctx, "w_lo", [P, 3, KD, D], F32R)
        rw_raw = sb(ctx, "rw_raw", [P, KD, E], F32)
        nw_col = sb(ctx, "nw_col", [P, KD], F32)
        rw = sb(ctx, "rw", [P, KD, 2 * E], F32R)
        b_col = sb(ctx, "b_col", [P, 2, G], F32)
        bv_row = sb(ctx, "bv_row", [P, D], F32)
        al_raw = sb(ctx, "al_raw", [H, CH], F32)
        al = sb(ctx, "al", [H, 2, CH], F32R)
        xs = sb(ctx, "xs", [P, 2, TPC, D], F32)
        x_hi = sb(ctx, "x_hi", [P, 2, KD, CH], F32R)
        x_lo = sb(ctx, "x_lo", [P, 2, KD, CH], F32R)
        qk_hi = sb(ctx, "qk_hi", [P, QK_RING, CH], F32R)
        qk_lo = sb(ctx, "qk_lo", [P, QK_RING, CH], F32R)
        squares = sb(ctx, "squares", [P, D], F32)
        stats = sb(ctx, "stats", [P, TPC, 6], F32)
        mv = sb(ctx, "mv", [P, TPC, 2], F32)
        ve = sb(ctx, "ve", [P, TPC], F32)
        sd = sb(ctx, "sd", [P, TPC], F32)
        rstd = sb(ctx, "rstd", [P, TPC], F32)
        newton = sb(ctx, "newton", [P, TPC], F32)
        ssq = sb(ctx, "ssq", [P, TPC], F32)
        ms = sb(ctx, "ms", [P, TPC], F32)
        rsd = sb(ctx, "rsd", [P, TPC], F32)
        rms = sb(ctx, "rms", [P, 2, TPC], F32)
        halves = sb(ctx, "halves", [P, TPC, 2 * E], F32)
        logits = sb(ctx, "logits", [P, TPC, E], F32)
        pad = sb(ctx, "pad", [P, 1], F32)
        best = sb(ctx, "best", [P, TPC, 8], F32)
        best_at = sb(ctx, "best_at", [P, TPC, 8], U32)
        xt = ps(ctx, "xt", [P, 2, CH])
        pj = ps(ctx, "pj", [P, BANKS, CH])
        pr = ps(ctx, "pr", [P, CH])

        small_loaded = sem(ctx, "small_loaded")
        w_raw_loaded = sem(ctx, "w_raw_loaded")
        w_hi_done = sem(ctx, "w_hi_done")
        w_split = sem(ctx, "w_split")
        rw_ready = sem(ctx, "rw_ready")
        x_loaded = [sem(ctx, f"x_loaded{p}") for p in range(2)]
        ve_ready = sem(ctx, "ve_ready")
        sd_ready = sem(ctx, "sd_ready")
        xn_ready = sem(ctx, "xn_ready")
        ssq_ready = sem(ctx, "ssq_ready")
        ms_ready = sem(ctx, "ms_ready")
        rsd_ready = sem(ctx, "rsd_ready")
        xt_ready = sem(ctx, "xt_ready")
        xh_ready = sem(ctx, "xh_ready")
        xl_ready = sem(ctx, "xl_ready")
        pj_ready = sem(ctx, "pj_ready")
        qk_hi_ready = sem(ctx, "qk_hi_ready")
        pj_used = sem(ctx, "pj_used")
        r_ready = sem(ctx, "r_ready")
        r_used = sem(ctx, "r_used")
        xn_stored = [sem(ctx, f"xn_stored{p}") for p in range(2)]
        qk_stored = [sem(ctx, f"qk_stored{p}") for p in range(QK_RING)]
        al_loaded = sem(ctx, "al_loaded")
        al_hi_ready = sem(ctx, "al_hi_ready")
        al_ready = sem(ctx, "al_ready")
        al_stored = sem(ctx, "al_stored")
        dve_step = sem(ctx, "dve_step")
        N_SMALL = 10
        block = ctx.enter_context(nc.Block())

        def x_rows(c):
            return x[bass.ds(c * CH, CH), :].rearrange("(j p) d -> p j d", p=P)

        @block.sync
        def _(sp):
            sp.dma_start(xs[:, 0], x_rows(0)).then_inc(x_loaded[0], 16)
            for dst, src in ((consts[:, :, :], t["cst"].rearrange("p (a n) -> p a n", a=5)),
                             (rw_raw[:, :, :], t["rwT"].rearrange("p (k e) -> p k e", k=KD)),
                             (nw_col[:, :], t["nw"]),
                             (b_col[:, 0], t["bq"]),
                             (b_col[:, 1], t["bk"]),
                             (bv_row[:, :], t["bv"].partition_broadcast(P)),
                             (t["rows_c"][:, :], t["rows"]),
                             (t["list_d"].rearrange("(p n) o -> p (n o)", p=P), t["no_pairs"]),
                             (t["xn_d"][T:T + P, :], t["no_rows"]),
                             (t["out"][T:T + P, :], t["no_rows"])):
                sp.dma_start(dst, src).then_inc(small_loaded, 16)
            for w, name in enumerate(("Wq", "Wk", "Wv")):
                if w:
                    sp.wait_ge(w_split, w)
                sp.dma_start(w_raw[:, :, :], t[name].rearrange("(k p) n -> p k n", p=P)).then_inc(w_raw_loaded, 16)
                if w == 0:
                    sp.dma_start(xs[:, 1], x_rows(1)).then_inc(x_loaded[1], 16)
            for a in range(S // CH):
                if a:
                    sp.wait_ge(al_ready, a)
                sp.dma_start(al_raw[:, :], t["alibi"][:, a * CH:(a + 1) * CH]).then_inc(al_loaded, 16)
                sp.wait_ge(al_ready, a + 1)
                sp.dma_start(t["bias_d"][:, :, a * CH:(a + 1) * CH], al[:, :, :].bitcast(F32)).then_inc(al_stored, 16)

            def chunk(c, par, load):
                sp.wait_ge(xn_ready, TPC * (c + 1))
                sp.dma_start(t["xn_d"][bass.ds(c * CH, CH), :].rearrange("(j p) d -> p j d", p=P),
                             xs[:, par]).then_inc(xn_stored[par], 16)
                for g in range(2 * G):
                    sp.wait_ge(pj_used, BANKS + NJ * c + g + 1)
                    hi_d, lo_d = (t["q_hi_d"], t["q_lo_d"]) if g < G else (t["k_hi_d"], t["k_lo_d"])
                    rows = slice((g % G) * P, (g % G + 1) * P)
                    cols = bass.ds((c % (NCH // B)) * CH, CH)
                    for d, s in ((hi_d, qk_hi), (lo_d, qk_lo)):
                        dst = d[bass.ds(c // (NCH // B), 1), rows, cols].rearrange("a r n -> (a r) n")
                        sp.dma_start(dst, s[:, g % QK_RING].bitcast(F32)).then_inc(qk_stored[g % QK_RING], 16)
                    if load and g == 0:
                        sp.wait_ge(ssq_ready, 1 + TPC * (c + 1))
                        sp.wait_ge(xt_ready, KD * (c + 1))
                        sp.wait_ge(xn_stored[par], 16 * (c // 2 + 1))
                        sp.dma_start(xs[:, par], x_rows(c + 2)).then_inc(x_loaded[par], 16)

            with nc.sync.Fori(0, NCH // 2 - 1) as i:
                chunk(2 * i, 0, True)
                chunk(2 * i + 1, 1, True)
            chunk(NCH - 2, 0, False)
            chunk(NCH - 1, 1, False)
            sp.wait_ge(small_loaded, 16 * N_SMALL)
            sp.wait_ge(al_stored, 16 * (S // CH))
            for p in range(2):
                sp.wait_ge(xn_stored[p], 16 * NCH // 2)
            for p in range(QK_RING):
                sp.wait_ge(qk_stored[p], 32 + 32 * 2 * G // QK_RING * NCH)

        @block.gpsimd
        def _(pool):
            for a in range(S // CH):
                pool.wait_ge(al_loaded, 16 * (a + 1))
                if a:
                    pool.wait_ge(al_stored, 16 * a)
                nc.gpsimd.tensor_copy(al[:, 0], al_raw[:, :]).then_inc(al_hi_ready, 1)
                pool.wait_ge(al_hi_ready, a + 1)
                nc.gpsimd.tensor_tensor(al[:, 1], al_raw[:, :], al[:, 0].bitcast(F32), ALU.subtract).then_inc(al_ready, 1)

        @block.scalar
        def _(act):
            def w_high(w):
                act.wait_ge(w_raw_loaded, 16 * (w + 1))
                nc.scalar.activation(w_hi[:, w], w_raw[:, :, :], ACT.Copy).then_inc(w_hi_done, 1)

            def deviation(c):
                act.wait_ge(ve_ready, c + 1)
                nc.scalar.activation(sd[:, :], ve[:, :], ACT.Sqrt).then_inc(sd_ready, 1)

            def square_sums(c, par):
                for j in range(TPC):
                    act.wait_ge(xn_ready, TPC * c + j + 1)
                    act.wait_ge(ssq_ready, TPC * c + j + 1)
                    nc.scalar.activation(squares[:, :], xs[:, par, j], ACT.Square,
                                         accum_out=ssq[:, j:j + 1]).then_inc(ssq_ready, 1)

            def router_root(c):
                act.wait_ge(ms_ready, c + 1)
                nc.scalar.activation(rsd[:, :], ms[:, :], ACT.Sqrt).then_inc(rsd_ready, 1)

            def x_high(c, par, k):
                act.wait_ge(xt_ready, KD * c + k + 1)
                nc.scalar.activation(x_hi[:, par, k], xt[:, k % 2], ACT.Copy).then_inc(xh_ready, 1)

            def qk_high(c, g):
                act.wait_ge(pj_ready, NJ * c + g + 1)
                act.wait_ge(qk_stored[g % QK_RING], 32 * (2 * G // QK_RING * c + g // QK_RING + 1))
                nc.scalar.activation(qk_hi[:, g % QK_RING], pj[:, g % BANKS], ACT.Identity,
                                     bias=b_col[:, g // G, g % G:g % G + 1]).then_inc(qk_hi_ready, 1)

            act.sem_inc(ssq_ready, 1)
            for p in range(QK_RING):
                act.sem_inc(qk_stored[p], 32)
            deviation(0)
            square_sums(0, 0)
            router_root(0)
            act.wait_ge(small_loaded, 16 * N_SMALL)
            w_high(0)
            for k in range(KD):
                x_high(0, 0, k)
            w_high(1)
            w_high(2)

            def chunk(c, par, ahead):
                for g in range(2 * G):
                    if ahead and g >= G:
                        x_high(c + 1, 1 - par, g - G)
                    qk_high(c, g)
                    if ahead and g == 0:
                        deviation(c + 1)
                    if ahead and g == 2:
                        square_sums(c + 1, 1 - par)
                    if ahead and g == G:
                        router_root(c + 1)

            with nc.scalar.Fori(0, NCH // 2 - 1) as i:
                chunk(2 * i, 0, True)
                chunk(2 * i + 1, 1, True)
            chunk(NCH - 2, 0, True)
            chunk(NCH - 1, 1, False)

        @block.vector
        def _(dve):
            step = Links(dve, dve_step)

            def inverse_root(out, var, root):
                step(nc.vector.reciprocal(out, root))
                step(nc.vector.tensor_tensor(newton[:, :], out, out, ALU.mult))
                step(nc.vector.tensor_tensor(newton[:, :], newton[:, :], var, ALU.mult))
                step(nc.vector.tensor_scalar(newton[:, :], newton[:, :], -0.5, 1.5, ALU.mult, ALU.add))
                step(nc.vector.tensor_tensor(out, out, newton[:, :], ALU.mult))

            def norm_stats(c, par):
                dve.wait_ge(x_loaded[par], 16 * (c // 2 + 1))
                for j in range(TPC):
                    last = nc.vector.bn_stats(stats[:, j], xs[:, par, j])
                step(last)
                nc.vector.memset(pad[:, :], 0.0)
                for j in range(TPC):
                    last = nc.vector.bn_aggr(mv[:, j], stats[:, j])
                step(last)
                nc.vector.tensor_scalar(ve[:, :], mv[:, :, 1], LN_EPS, None, ALU.add).then_inc(ve_ready, 1)

            def normalise(c, par):
                dve.wait_ge(sd_ready, c + 1)
                inverse_root(rstd[:, :], ve[:, :], sd[:, :])
                for j in range(TPC):
                    nc.vector.tensor_scalar(xs[:, par, j], xs[:, par, j], mv[:, j, 0:1], rstd[:, j:j + 1],
                                            ALU.subtract, ALU.mult).then_inc(xn_ready, 1)

            def mean_square(c):
                dve.wait_ge(ssq_ready, 1 + TPC * (c + 1))
                nc.vector.tensor_scalar(ms[:, :], ssq[:, :], 1.0 / D, RMS_EPS, ALU.mult, ALU.add).then_inc(ms_ready, 1)

            def router_scale(c, par):
                dve.wait_ge(rsd_ready, c + 1)
                inverse_root(rms[:, par], ms[:, :], rsd[:, :])

            def w_low(w):
                dve.wait_ge(w_hi_done, w + 1)
                nc.vector.tensor_tensor(w_lo[:, w], w_raw[:, :, :], w_hi[:, w].bitcast(F32),
                                        ALU.subtract).then_inc(w_split, 1)

            def x_low(c, par, k):
                dve.wait_ge(xh_ready, KD * c + k + 1)
                nc.vector.tensor_tensor(x_lo[:, par, k], xt[:, k % 2], x_hi[:, par, k].bitcast(F32),
                                        ALU.subtract).then_inc(xl_ready, 1)

            def qk_low(c, g):
                dve.wait_ge(qk_hi_ready, 2 * G * c + g + 1)
                nc.vector.scalar_tensor_tensor(qk_lo[:, g % QK_RING], pj[:, g % BANKS], b_col[:, g // G, g % G:g % G + 1],
                                               qk_hi[:, g % QK_RING].bitcast(F32), ALU.add,
                                               ALU.subtract).then_inc(pj_used, 1)

            def keep_values(c, j):
                dve.wait_ge(pj_ready, NJ * c + 2 * G + j + 1)
                nc.vector.tensor_tensor(values[:, bass.ds((TPC * c + j) * D, D)], pj[:, j % BANKS], bv_row[:, :],
                                        ALU.add).then_inc(pj_used, 1)

            def route(c, par):
                dve.wait_ge(r_ready, c + 1)
                nc.vector.tensor_copy(halves[:, :, :], pr[:, 0:TPC * 2 * E].rearrange("p (j e) -> p j e", j=TPC)).then_inc(r_used, 1)
                dve.wait_ge(r_used, c + 2)
                step(nc.vector.tensor_tensor(logits[:, :, :], halves[:, :, 0:E], halves[:, :, E:2 * E], ALU.add))
                step(nc.vector.tensor_tensor(logits[:, :, :], logits[:, :, :],
                                             rms[:, par].unsqueeze(2).to_broadcast([P, TPC, E]), ALU.mult))
                nc.vector.memset(pad[:, :], 0.0)
                for j in range(TPC):
                    last = nc.vector.max(best[:, j], logits[:, j])
                step(last)
                nc.vector.memset(pad[:, :], 0.0)
                for j in range(TPC):
                    last = nc.vector.max_index(best_at[:, j], best[:, j], logits[:, j])
                step(last)
                nc.vector.tensor_copy(top_val[:, bass.ds(TPC * c, TPC), :], best[:, :, :])
                step(nc.vector.tensor_copy(top_idx[:, bass.ds(TPC * c, TPC), :], best_at[:, :, :]))

            dve.sem_inc(xl_ready, 2)
            dve.sem_inc(pj_used, BANKS)
            dve.sem_inc(r_used, 1)
            norm_stats(0, 0)
            normalise(0, 0)
            mean_square(0)
            dve.wait_ge(small_loaded, 16 * N_SMALL)
            nc.vector.tensor_copy(mask_r[:, :, :], consts[:, 0:3, :])
            for k in range(KD):
                last = nc.vector.tensor_scalar(rw_raw[:, k], rw_raw[:, k], nw_col[:, k:k + 1], None, ALU.mult)
            step(last)
            step(nc.vector.tensor_copy(rw[:, :, 0:E], rw_raw[:, :, :]))
            nc.vector.tensor_tensor(rw[:, :, E:2 * E], rw_raw[:, :, :], rw[:, :, 0:E].bitcast(F32),
                                    ALU.subtract).then_inc(rw_ready, 1)
            router_scale(0, 0)
            w_low(0)
            for k in range(KD):
                x_low(0, 0, k)
            w_low(1)
            w_low(2)

            def chunk(c, par, ahead):
                if ahead:
                    norm_stats(c + 1, 1 - par)
                for g in range(2 * G):
                    if ahead and g >= G:
                        x_low(c + 1, 1 - par, g - G)
                    qk_low(c, g)
                    if ahead and g == 0:
                        normalise(c + 1, 1 - par)
                    if ahead and g == G - 1:
                        mean_square(c + 1)
                    if ahead and g == G:
                        router_scale(c + 1, 1 - par)
                for j in range(TPC):
                    keep_values(c, j)
                route(c, par)

            start = step.n
            with nc.vector.Fori(0, NCH // 2 - 1) as i:
                step.base, step.n = start + i * STEPS_PER_PAIR, 0
                chunk(2 * i, 0, True)
                chunk(2 * i + 1, 1, True)
                assert step.n == STEPS_PER_PAIR, step.n
            step.base, step.n = start + (NCH // 2 - 1) * STEPS_PER_PAIR, 0
            chunk(NCH - 2, 0, True)
            chunk(NCH - 1, 1, False)

        @block.tensor
        def _(pe):
            def transpose_x(c, par, k):
                pe.wait_ge(xn_ready, TPC * (c + 1))
                pe.wait_ge(xl_ready, KD * c + k + 1)
                for j in range(TPC):
                    last = nc.tensor.transpose(xt[:, k % 2, j * P:(j + 1) * P], xs[:, par, j, k * P:(k + 1) * P], ident)
                last.then_inc(xt_ready, 1)

            def tile(c, g, pairs):
                pe.wait_ge(pj_used, NJ * c + g + 1)
                for k in range(KD):
                    for n, (lhsT, rhs) in enumerate(pairs(k)):
                        last = nc.tensor.matmul(pj[:, g % BANKS], lhsT, rhs, start=(k == 0 and n == 0),
                                                stop=(k == KD - 1 and n == 2))
                last.then_inc(pj_ready, 1)

            def qk_tile(c, par, g):
                w, cols = g // G, slice((g % G) * P, (g % G + 1) * P)
                tile(c, g, lambda k: ((w_hi[:, w, k, cols], x_hi[:, par, k]), (w_hi[:, w, k, cols], x_lo[:, par, k]),
                                      (w_lo[:, w, k, cols], x_hi[:, par, k])))

            def v_tile(c, par, j):
                rows = slice(j * P, (j + 1) * P)
                tile(c, 2 * G + j, lambda k: ((x_hi[:, par, k, rows], w_hi[:, 2, k]), (x_hi[:, par, k, rows], w_lo[:, 2, k]),
                                              (x_lo[:, par, k, rows], w_hi[:, 2, k])))

            def router_tiles(c, par):
                pe.wait_ge(r_used, c + 1)
                for j in range(TPC):
                    rows = slice(j * P, (j + 1) * P)
                    for k in range(KD):
                        for n, part in enumerate((x_hi, x_lo)):
                            last = nc.tensor.matmul(pr[:, 2 * E * j:2 * E * (j + 1)], part[:, par, k, rows], rw[:, k],
                                                    start=(k == 0 and n == 0), stop=(k == KD - 1 and n == 1))
                last.then_inc(r_ready, 1)

            pe.wait_ge(small_loaded, 16 * N_SMALL)
            pe.wait_ge(rw_ready, 1)
            for k in range(KD):
                transpose_x(0, 0, k)

            def chunk(c, par, ahead):
                pe.wait_ge(xl_ready, 2 + KD * (c + 1))
                pe.wait_ge(w_split, 1)
                for g in range(2 * G):
                    if g == G:
                        pe.wait_ge(w_split, 2)
                    if ahead and g >= G:
                        transpose_x(c + 1, 1 - par, g - G)
                    qk_tile(c, par, g)
                pe.wait_ge(w_split, 3)
                for j in range(TPC):
                    v_tile(c, par, j)
                router_tiles(c, par)

            with nc.tensor.Fori(0, NCH // 2 - 1) as i:
                chunk(2 * i, 0, True)
                chunk(2 * i + 1, 1, True)
            chunk(NCH - 2, 0, True)
            chunk(NCH - 1, 1, False)


def attend(nc, sb, ps, sem, t):
    ident, ident_r, mask_m, mask_s = t["ident"], t["ident_r"], t["mask_m"], t["mask_s"]
    values = t["values"]
    with ExitStack() as ctx:
        k_st = sb(ctx, "k_st", [P, HEADS_RING, S], F32R)
        q_st = sb(ctx, "q_st", [P, HEADS_RING, S], F32R)
        v_split = sb(ctx, "v_split", [P, HEADS_RING, QT, VS], F32R)
        v_whole = sb(ctx, "v_whole", [P, HEADS_RING, QT // TPC, 2 * HD], F32)
        probs = sb(ctx, "probs", [P, P_RING, CH], F32)
        probs_hi = sb(ctx, "probs_hi", [P, P_RING, CH], F32R)
        probs_lo = sb(ctx, "probs_lo", [P, P_RING, CH], F32R)
        high_sums = sb(ctx, "high_sums", [2 * HD, 2, CH], F32)
        low_sums = sb(ctx, "low_sums", [HD, 2, CH], F32)
        m_part = sb(ctx, "m_part", [P, M_PARTS, QT], F32)
        m_max = sb(ctx, "m_max", [P, QT], F32)
        m_neg = sb(ctx, "m_neg", [P, QT], F32)
        m_rows = sb(ctx, "m_rows", [QT, 2, P], F32R)
        idx_f = sb(ctx, "idx_f", [P, TT, TOP_K], F32)
        hot = sb(ctx, "hot", [P, TOP_K, TT, E], F32)
        both = sb(ctx, "both", [P, TT, E], F32)
        counts = sb(ctx, "counts", [P, 2, TT, E], F32)
        so_far = sb(ctx, "so_far", [P, TT, E], F32)
        padded_i = sb(ctx, "padded_i", [P, E], I32)
        padded = sb(ctx, "padded", [P, E], F32)
        ends = sb(ctx, "ends", [P, E], F32)
        starts = sb(ctx, "starts", [P, E], F32)
        base = sb(ctx, "base", [P, TT, E], F32)
        slot_f = sb(ctx, "slot_f", [P, TT, TOP_K], F32)
        slot_tile_i = sb(ctx, "slot_tile_i", [P, TT, TOP_K], I32)
        slot_tile = idx_f
        passed = sb(ctx, "passed", [1, NMT + 1, E], F32)
        te_f = sb(ctx, "te_f", [1, NMT + 1], F32)
        gap = sb(ctx, "gap", [P, TT], F32)
        ratio = sb(ctx, "ratio", [P, TT], F32)
        denom = sb(ctx, "denom", [P, TT], F32)
        pairs = sb(ctx, "pairs", [P, TT, TOP_K, 2], I32)

        m_ps = ps(ctx, "m_ps", [P, M_BUFS, M_WIDE])
        s_ps = ps(ctx, "s_ps", [P, S_BUFS, CH])
        o_ps = ps(ctx, "o_ps", [P, 2, CH])

        k_ones = sem(ctx, "k_ones")
        q_ones = sem(ctx, "q_ones")
        q_more_ones = sem(ctx, "q_more_ones")
        st_loaded = [sem(ctx, f"st_loaded{p}") for p in range(HEADS_RING)]
        s_ready = sem(ctx, "s_ready")
        p_ready = sem(ctx, "p_ready")
        pv_done = sem(ctx, "pv_done")
        m_scored = sem(ctx, "m_scored")
        m_taken = sem(ctx, "m_taken")
        m_rows_ready = sem(ctx, "m_rows_ready")
        m_placed = sem(ctx, "m_placed")
        high_by_dve = sem(ctx, "high_by_dve")
        lo_ready_dve = sem(ctx, "lo_ready_dve")
        lo_ready_pool = sem(ctx, "lo_ready_pool")
        o_copied = sem(ctx, "o_copied")
        o_added = sem(ctx, "o_added")
        ctx_stored = [sem(ctx, f"ctx_stored{p}") for p in range(2)]
        v_ones = sem(ctx, "v_ones")
        v_high_ready = sem(ctx, "v_high_ready")
        v_ready = sem(ctx, "v_ready")
        counts_taken = sem(ctx, "counts_taken")
        hot_ready = sem(ctx, "hot_ready")
        counted = sem(ctx, "counted")
        gap_ready = sem(ctx, "gap_ready")
        ratio_ready = sem(ctx, "ratio_ready")
        ids_loaded = sem(ctx, "ids_loaded")
        slots_ready = sem(ctx, "slots_ready")
        listed = sem(ctx, "listed")
        dve_step = sem(ctx, "dve_step2")
        ST_DMAS = 7
        QCS = S // CH
        block = ctx.enter_context(nc.Block())

        def low_operands(u):
            w = s_span(u)[1]
            return (probs_lo[:, u % P_RING, 0:w], probs[:, u % P_RING, 0:w], probs_hi[:, u % P_RING, 0:w].bitcast(F32))

        def high_count(n, u):
            return sum(HIGH_ON_DVE) * n + sum(HIGH_ON_DVE[:u + 1])

        def transposed(d, n):
            return d[bass.ds(n // H, 1), bass.ds((n % H) * HD, HD), :].rearrange("a r n -> (a r) n")

        @block.sync
        def _(sp):
            sp.dma_start(pairs[:, :, :, :].rearrange("p a k c -> p (a k c)"), t["token_pairs"]).then_inc(ids_loaded, 16)

            def load(n, r, first=False):
                k_hi, k_lo = transposed(t["k_hi_d"], n), transposed(t["k_lo_d"], n)
                q_hi, q_lo = transposed(t["q_hi_d"], n), transposed(t["q_lo_d"], n)
                bias = t["bias_d"][bass.ds(n % H, 1), :, :].rearrange("a r n -> (a r) n")
                for dst, at, src in ((k_st, 0, k_hi), (q_st, 0, q_hi), (k_st, 32, k_hi), (q_st, 32, q_lo),
                                     (k_st, 64, k_lo), (q_st, 64, q_hi)):
                    sp.dma_start(dst[at:at + HD, r, :].bitcast(F32), src).then_inc(st_loaded[r], 16)
                if first:
                    sp.wait_ge(k_ones, r + 1)
                sp.dma_start(k_st[ROW_BIAS:ROW_BIAS + 2, r, :].bitcast(F32), bias).then_inc(st_loaded[r], 16)

            def place_maxima(n, r):
                sp.wait_ge(m_rows_ready, n + 1)
                for part in range(2):
                    dst = q_st[ROW_MAX + part:ROW_MAX + part + 1, r, :].bitcast(F32).rearrange("o (a b) -> o a b", a=QT)
                    sp.dma_start(dst, m_rows[:, part, :].bitcast(F32)).then_inc(m_placed, 16)

            def store_context(n, qc):
                sp.wait_ge(o_added, 2 + QCS * n + qc + 1)
                at = slice(qc * CH, (qc + 1) * CH)
                sp.dma_start(t["ctx_d"][bass.ds(n * HD, HD), at], high_sums[0:HD, qc % 2, :]).then_inc(ctx_stored[qc % 2], 16)
                sp.dma_start(t["weight_sums_d"][bass.ds(n, 1), at], high_sums[HD:HD + 1, qc % 2, :]).then_inc(ctx_stored[qc % 2], 16)

            load(0, 0, first=True)
            load(1, 1, first=True)
            sp.wait_ge(q_ones, 1)
            place_maxima(0, 0)
            sp.wait_ge(k_ones, HEADS_RING)
            sp.wait_ge(q_more_ones, HEADS_RING - 1)

            def step_n(n, r, load_ahead=True, maxima=True, before=True):
                if load_ahead:
                    if before:
                        sp.wait_ge(pv_done, P_RING + NS * n)
                    load((n + 2) % NH, (r + 2) % HEADS_RING)
                for kind, u, back in ATTEND:
                    if kind == "O" and (before or not back):
                        store_context(n - back, u)
                    if maxima and kind == "W":
                        place_maxima(n + 1, (r + 1) % HEADS_RING)

            step_n(0, 0, before=False)
            with nc.sync.Fori(0, LOOPS) as i:
                for k in range(1, HEADS_RING + 1):
                    step_n(HEADS_RING * i + k, k % HEADS_RING)
            step_n(NH - 1, (NH - 1) % HEADS_RING, load_ahead=False, maxima=False)
            store_context(NH - 1, QCS - 1)
            for p in range(2):
                sp.wait_ge(ctx_stored[p], 32 + 32 * NH * QCS // 2)
            for r in range(HEADS_RING):
                sp.wait_ge(st_loaded[r], 16 * ST_DMAS * len(range(r, NH + 1, HEADS_RING)))
            sp.wait_ge(m_placed, 32 * NH)
            sp.wait_ge(ids_loaded, 16)

        @block.gpsimd
        def _(pool):
            for r in range(HEADS_RING):
                nc.gpsimd.memset(k_st[ROW_BIAS:P, r, :].bitcast(F32), 1.0).then_inc(k_ones, 1)
            for r in range(1, HEADS_RING):
                nc.gpsimd.memset(q_st[ROW_BIAS:P, r, :].bitcast(F32), 1.0).then_inc(q_more_ones, 1)
            pool.wait_ge(k_ones, HEADS_RING)
            pool.wait_ge(q_more_ones, HEADS_RING - 1)
            nc.gpsimd.memset(v_split[:, :, :, HD:2 * HD].bitcast(F32), 1.0)
            nc.gpsimd.memset(v_whole[:, :, :, HD:2 * HD], 1.0).then_inc(v_ones, 1)

            def low_part(n, u):
                if HIGH_ON_DVE[u]:
                    pool.wait_ge(high_by_dve, high_count(n, u))
                else:
                    pool.wait_ge(p_ready, S_BUFS + NS * n + u + 1)
                nc.gpsimd.tensor_tensor(*low_operands(u), ALU.subtract).then_inc(lo_ready_pool, 1)

            def list_tokens(tiles):
                for a in tiles:
                    for k in range(TOP_K):
                        nc.gpsimd.indirect_dma_start(
                            out=t["list_d"], out_offset=bass.IndirectOffsetOnAxis(ap=t["slot"][:, a, k:k + 1], axis=0),
                            in_=pairs[:, a, k, :], in_offset=None).then_inc(listed, 16)

            def add_sums(n, qc):
                pool.wait_ge(o_copied, 2 + QCS * n + qc + 1)
                high = high_sums[0:HD, qc % 2, :]
                nc.gpsimd.tensor_tensor(high, high, low_sums[:, qc % 2, :], ALU.add).then_inc(o_added, 1)

            def step_n(n, edge=False, tiles=(), before=True):
                for kind, u, back in ATTEND:
                    if back and not before:
                        continue
                    if kind == "L" and ((EDGE_ON_POOL if edge and not back else ON_POOL)[u]):
                        low_part(n - back, u)
                    if kind == "O":
                        add_sums(n - back, u)
                    if kind == "O" and tiles:
                        list_tokens(tiles[:5])
                        tiles = tiles[5:]

            pool.wait_ge(slots_ready, 1)
            first = TT // 2 + 3
            list_tokens(range(0, 5))
            step_n(0, edge=True, tiles=range(5, first), before=False)
            with nc.gpsimd.Fori(0, LOOPS) as i:
                for k in range(1, HEADS_RING + 1):
                    step_n(HEADS_RING * i + k)
            step_n(NH - 1, edge=True, tiles=range(first, TT))
            for kind, u, back in ATTEND:
                if back and kind == "L" and ON_POOL[u]:
                    low_part(NH - 1, u)
            add_sums(NH - 1, QCS - 1)
            pool.wait_ge(listed, 16 * TT * TOP_K)

        @block.scalar
        def _(act):
            act.sem_inc(p_ready, S_BUFS)
            for p in range(2):
                act.sem_inc(ctx_stored[p], 32)
            act.sem_inc(o_copied, 2)
            act.sem_inc(o_added, 2)
            act.wait_ge(gap_ready, 1)
            nc.scalar.activation(ratio[:, :], gap[:, :], ACT.Exp).then_inc(ratio_ready, 1)

            def weights(n, u):
                w = s_span(u)[1]
                act.wait_ge(s_ready, NS * n + u + 1)
                act.wait_ge(pv_done, NS * n + u + 1)
                scores = s_ps[:, u % S_BUFS, CH - w:CH]
                if SPLIT[u] and not HIGH_ON_DVE[u]:
                    nc.scalar.activation(probs_hi[:, u % P_RING, 0:w], scores, ACT.Exp, scale=SCALE)
                nc.scalar.activation(probs[:, u % P_RING, 0:w], scores, ACT.Exp, scale=SCALE).then_inc(p_ready, 1)

            def take_sums(n, qc):
                act.wait_ge(pv_done, P_RING + NS * n + LAST_UNIT[qc] + 1)
                act.wait_ge(ctx_stored[qc % 2], 32 * (QCS // 2 * n + qc // 2 + 1))
                nc.scalar.activation(high_sums[:, qc % 2, :], o_ps[0:2 * HD, qc % 2, :], ACT.Copy)
                act.wait_ge(o_added, QCS * n + qc + 1)
                nc.scalar.activation(low_sums[:, qc % 2, :], o_ps[2 * HD:VS, qc % 2, :], ACT.Copy).then_inc(o_copied, 1)

            def step_n(n, before=True):
                for kind, u, back in ATTEND:
                    if kind == "S":
                        weights(n, u)
                    if kind == "O" and (before or not back):
                        take_sums(n - back, u)

            step_n(0, before=False)
            with nc.scalar.Fori(1, NH) as n:
                step_n(n)
            take_sums(NH - 1, QCS - 1)

        @block.vector
        def _(dve):
            step = Links(dve, dve_step)
            V = nc.vector

            def take_maximum(n, m):
                qt, part = M_UNITS[m]
                w = m_span(m)[1]
                dve.wait_ge(m_scored, M_SLOTS * n + m + 1)
                V.tensor_reduce(m_part[:, part, qt:qt + 1], m_ps[:, m % M_BUFS, 0:w], AX.X, ALU.max).then_inc(m_taken, 1)

            def fold_maxima(n):
                dve.wait_ge(m_taken, M_SLOTS * n + NM)
                step(V.tensor_reduce(m_max[:, :], m_part[:, :, :].rearrange("p a q -> p q a"), AX.X, ALU.max))
                V.tensor_scalar(m_neg[:, :], m_max[:, :], -1.0, None, ALU.mult).then_inc(m_taken, 1)

            def maxima_rows(n, placed_before):
                dve.wait_ge(m_scored, M_SLOTS * n + NM + 1)
                if placed_before:
                    dve.wait_ge(m_placed, 32 * n)
                src = m_ps[0:QT, NM % M_BUFS, 0:P]
                step(V.tensor_copy(m_rows[:, 0], src))
                V.tensor_tensor(m_rows[:, 1], src, m_rows[:, 0].bitcast(F32), ALU.subtract).then_inc(m_rows_ready, 1)

            def high_part(n, u):
                dve.wait_ge(p_ready, S_BUFS + NS * n + u + 1)
                w = s_span(u)[1]
                V.tensor_copy(probs_hi[:, u % P_RING, 0:w], probs[:, u % P_RING, 0:w]).then_inc(high_by_dve, 1)

            def low_part(n, u):
                if HIGH_ON_DVE[u]:
                    dve.wait_ge(high_by_dve, high_count(n, u))
                else:
                    dve.wait_ge(p_ready, S_BUFS + NS * n + u + 1)
                V.tensor_tensor(*low_operands(u), ALU.subtract).then_inc(lo_ready_dve, 1)

            def stack_values(n, r, part, count):
                src = by_tile[:, bass.ds((n // H) * QT, QT), bass.ds(n % H, 1), :].rearrange("p t a w -> p t (a w)")
                chunk_ends = src.rearrange("p (c j) w -> p c j w", j=TPC)[:, :, TPC - 1, :]
                if part == 0:
                    V.tensor_copy(v_whole[:, r, :, 0:HD], chunk_ends)
                    V.tensor_copy(v_split[:, r, :, 0:HD], src).then_inc(v_high_ready, 1)
                else:
                    dve.wait_ge(v_high_ready, count + 1)
                    V.tensor_tensor(v_split[:, r, :, 2 * HD:VS], src, v_split[:, r, :, 0:HD].bitcast(F32),
                                    ALU.subtract).then_inc(v_ready, 1)

            def place_tokens():
                numbers, firsts = t["rows_c"][:, 0:E], t["rows_c"][0:1, E:]
                top_val = t["top_val"]
                share = pairs[:, :, :, 1].bitcast(F32)
                V.tensor_tensor(gap[:, :], top_val[:, :, 1], top_val[:, :, 0], ALU.subtract).then_inc(gap_ready, 1)
                step(V.tensor_copy(idx_f[:, :, :], t["top_idx"][:, :, 0:TOP_K]))
                for k in range(TOP_K):
                    last = V.tensor_tensor(hot[:, k], idx_f[:, :, k:k + 1].to_broadcast([P, TT, E]),
                                           numbers.unsqueeze(1).to_broadcast([P, TT, E]), ALU.is_equal)
                step(last)
                V.tensor_tensor(both[:, :, :], hot[:, 0], hot[:, 1], ALU.add).then_inc(hot_ready, 1)
                dve.wait_ge(ratio_ready, 1)
                dve.wait_ge(ids_loaded, 16)
                step(V.tensor_scalar(denom[:, :], ratio[:, :], 1.0, None, ALU.add))
                step(V.reciprocal(denom[:, :], denom[:, :]))
                step(V.tensor_scalar(share[:, :, 0], denom[:, :], MOE_SCALE, None, ALU.mult))
                step(V.tensor_tensor(share[:, :, 1], share[:, :, 0], ratio[:, :], ALU.mult))
                dve.wait_ge(counted, 1)
                step(V.tensor_copy(counts[:, :, :, :], o_ps[:, 1, :].rearrange("p (a t e) -> p a t e", a=2, t=TT)))
                dve.sem_inc(counts_taken, 1)
                for e in range(E):
                    last = V.tensor_tensor_scan(so_far[:, :, e], t["ones"][:, 0:TT], counts[:, 1, :, e], 0.0,
                                                ALU.mult, ALU.add)
                step(last)
                step(V.tensor_scalar(padded_i[:, :], so_far[:, TT - 1, :], float(P - 1), None, ALU.add))
                shift = P.bit_length() - 1
                step(V.tensor_scalar(padded_i[:, :], padded_i[:, :], shift, shift, ALU.logical_shift_right,
                                     ALU.logical_shift_left))
                step(V.tensor_copy(padded[:, :], padded_i[:, :]))
                step(V.tensor_tensor_scan(ends[:, :], t["ones"][:, 0:E], padded[:, :], 0.0, ALU.mult, ALU.add))
                step(V.tensor_tensor(starts[:, :], ends[:, :], padded[:, :], ALU.subtract))
                step(V.tensor_tensor(base[:, :, :], so_far[:, :, :], counts[:, 1], ALU.subtract))
                step(V.tensor_tensor(base[:, :, :], base[:, :, :], counts[:, 0], ALU.add))
                step(V.tensor_tensor(base[:, :, :], base[:, :, :], starts[:, :].unsqueeze(1).to_broadcast([P, TT, E]), ALU.add))
                for k in range(TOP_K):
                    last = V.tensor_tensor(hot[:, k], hot[:, k], base[:, :, :], ALU.mult)
                step(last)
                for k in range(TOP_K):
                    last = V.tensor_reduce(slot_f[:, :, k], hot[:, k], AX.X, ALU.add)
                step(last)
                step(V.tensor_copy(slot_tile_i[:, :, :], slot_f[:, :, :]))
                step(V.tensor_scalar(slot_tile_i[:, :, :], slot_tile_i[:, :, :], shift, None, ALU.logical_shift_right))
                step(V.tensor_copy(slot_tile[:, :, :], slot_tile_i[:, :, :]))
                step(V.tensor_scalar(slot_f[:, :, :], slot_f[:, :, :], float(NMT), None, ALU.mult))
                step(V.tensor_scalar(slot_tile[:, :, :], slot_tile[:, :, :], float(P * NMT - 1), None, ALU.mult))
                V.tensor_tensor(t["slot"][:, :, :], slot_f[:, :, :], slot_tile[:, :, :], ALU.subtract).then_inc(slots_ready, 1)
                step(V.tensor_tensor(passed[:, :, :], firsts.unsqueeze(2).to_broadcast([1, NMT + 1, E]),
                                     ends[0:1, :].unsqueeze(1).to_broadcast([1, NMT + 1, E]), ALU.is_ge))
                step(V.tensor_reduce(te_f[:, :], passed[:, :, :], AX.X, ALU.add))
                V.tensor_scalar(t["tile_expert"][:, :], te_f[:, :], float(E - 1), None, ALU.min)

            by_tile = values[:, :].rearrange("p (t h w) -> p t h w", t=TT, h=H)
            V.memset(q_st[ROW_BIAS:P, 0, :].bitcast(F32), 1.0).then_inc(q_ones, 1)
            place_tokens()
            step(V.memset(m_part[:, :, :], NEG))
            for m in range(NM):
                take_maximum(0, m)
            fold_maxima(0)
            dve.wait_ge(v_ones, 1)
            for part in range(2):
                stack_values(0, 0, part, 0)
            maxima_rows(0, False)
            for part in range(2):
                stack_values(1, 1, part, 1)
            def step_n(n, r, maxima=True, edge=False, values=True, before=True):
                for kind, u, back in ATTEND:
                    if back and not before:
                        continue
                    if kind == "H":
                        high_part(n - back, u)
                    if kind == "C" and values:
                        if u == 0 and before:
                            dve.wait_ge(pv_done, P_RING + NS * n)
                        stack_values((n + 2) % NH, (r + 2) % HEADS_RING, u, n + 2)
                    if kind == "L" and not (EDGE_ON_POOL if edge and not back else ON_POOL)[u]:
                        low_part(n - back, u)
                    if maxima and kind == "M":
                        take_maximum(n + 1, u)
                    if maxima and kind == "X":
                        fold_maxima(n + 1)
                    if maxima and kind == "W":
                        maxima_rows(n + 1, True)

            step_n(0, 0, edge=True, before=False)
            start = step.n
            per = 2
            with nc.vector.Fori(0, LOOPS) as i:
                for k in range(1, HEADS_RING + 1):
                    n = HEADS_RING * i + k
                    step.base, step.n = start + (n - 1) * per, 0
                    step_n(n, k % HEADS_RING)
                    assert step.n == per, step.n
            step_n(NH - 1, (NH - 1) % HEADS_RING, maxima=False, edge=True, values=False)
            for kind, u, back in ATTEND:
                if back and kind == "H":
                    high_part(NH - 1, u)
                if back and kind == "L" and not ON_POOL[u]:
                    low_part(NH - 1, u)

        @block.tensor
        def _(pe):
            def maximum_tile(n, r, m, first=False):
                qt, part = M_UNITS[m]
                k0, w = m_span(m)
                if m >= M_BUFS:
                    pe.wait_ge(m_taken, M_SLOTS * n + m - M_BUFS + 1)
                elif not first:
                    pe.wait_ge(m_rows_ready, n)
                for c0 in range(0, w, CH):
                    cw = min(CH, w - c0)
                    diagonal = k0 + c0 + cw == (qt + 1) * P
                    last = nc.tensor.matmul(m_ps[:, m % M_BUFS, c0:c0 + cw], q_st[0:ROW_MAX, r, qt * P:(qt + 1) * P],
                                            k_st[0:ROW_MAX, r, k0 + c0:k0 + c0 + cw], start=True, stop=not diagonal)
                    if diagonal:
                        last = nc.tensor.matmul(m_ps[:, m % M_BUFS, c0 + cw - P:c0 + cw], ident_r, mask_m,
                                                start=False, stop=True)
                last.then_inc(m_scored, 1)

            def transpose_maxima(n):
                pe.wait_ge(m_taken, M_SLOTS * (n + 1))
                nc.tensor.transpose(m_ps[0:QT, NM % M_BUFS, 0:P], m_neg[:, :], ident).then_inc(m_scored, 1)

            def score_tile(n, r, u):
                qc, kt = S_UNITS[u]
                q0, w = s_span(u)
                more = max(0, 2 * P - w)
                diagonal = q0 == kt * P
                pe.wait_ge(p_ready, NS * n + u + 1)
                last = nc.tensor.matmul(s_ps[:, u % S_BUFS, CH - w - more:CH], k_st[0:ROWS, r, kt * P:(kt + 1) * P],
                                        q_st[0:ROWS, r, q0 - more:q0 + w], start=True, stop=not diagonal)
                if diagonal:
                    last = nc.tensor.matmul(s_ps[:, u % S_BUFS, CH - w:CH - w + P], ident_r, mask_s, start=False, stop=True)
                last.then_inc(s_ready, 1)

            def value_products(n, r, u, edge=False):
                qc, kt = S_UNITS[u]
                q0, w = s_span(u)
                if kt == 0:
                    pe.wait_ge(o_copied, QCS * n + qc + 1)
                at = slice(q0 - qc * CH, CH)
                place = u % P_RING
                if SPLIT[u]:
                    by_pool = (EDGE_ON_POOL if edge else ON_POOL)[u]
                    pe.wait_ge(lo_ready_pool if by_pool else lo_ready_dve, low_count(by_pool, n, u, edge))
                    nc.tensor.matmul(o_ps[0:VS, qc % 2, at], v_split[:, r, kt, :], probs_hi[:, place, 0:w],
                                     start=(kt == 0), stop=True, skip_group_check=True)
                    last = nc.tensor.matmul(o_ps[0:VS, qc % 2, at], v_split[:, r, kt, :], probs_lo[:, place, 0:w],
                                            start=False, stop=True, skip_group_check=True)
                else:
                    pe.wait_ge(p_ready, S_BUFS + NS * n + u + 1)
                    last = nc.tensor.matmul(o_ps[0:2 * HD, qc % 2, at], v_whole[:, r, qc, :], probs[:, place, 0:w],
                                            start=False, stop=True, skip_group_check=True)
                last.then_inc(pv_done, 1)

            pe.sem_inc(pv_done, P_RING)
            pe.wait_ge(hot_ready, 1)
            hot2 = both[:, :, :].rearrange("p t e -> p (t e)")
            nc.tensor.matmul(o_ps[:, 1, 0:TT * E], t["triu"], hot2, start=True, stop=True)
            nc.tensor.matmul(o_ps[:, 1, TT * E:2 * TT * E], t["ones"], hot2, start=True, stop=True).then_inc(counted, 1)
            pe.wait_ge(st_loaded[0], 16 * ST_DMAS)
            pe.wait_ge(q_ones, 1)
            for m in range(NM):
                maximum_tile(0, 0, m, first=True)
            transpose_maxima(0)
            pe.wait_ge(counts_taken, 1)
            pe.wait_ge(v_ones, 1)
            pe.wait_ge(q_more_ones, HEADS_RING - 1)

            def step_n(n, r, st_round=None, edge=False, before=True):
                maxima = st_round is not None
                r1 = (r + 1) % HEADS_RING
                pe.wait_ge(m_placed, 32 * (n + 1))
                pe.wait_ge(v_ready, n + 1)
                if maxima:
                    pe.wait_ge(st_loaded[r1], 16 * ST_DMAS * st_round)
                for kind, u, back in ATTEND:
                    if kind == "S":
                        score_tile(n, r, u)
                    if kind == "V" and not back:
                        value_products(n, r, u, edge)
                    if kind == "V" and back and before:
                        value_products(n - 1, (r - 1) % HEADS_RING, u)
                    if maxima and kind == "M":
                        maximum_tile(n + 1, r1, u)
                    if maxima and kind == "W":
                        transpose_maxima(n + 1)

            step_n(0, 0, st_round=1, edge=True, before=False)
            with nc.tensor.Fori(0, LOOPS) as i:
                for k in range(1, HEADS_RING + 1):
                    step_n(HEADS_RING * i + k, k % HEADS_RING, st_round=i + (k + 1) // HEADS_RING + 1)
            step_n(NH - 1, (NH - 1) % HEADS_RING, edge=True)
            for kind, u, back in ATTEND:
                if back and kind == "V":
                    value_products(NH - 1, (NH - 1) % HEADS_RING, u, edge=True)


def output(nc, sb, ps, sem, t):
    UW = 2 * P
    TPU = UW // P
    NU = T // UW
    X_RING = 4
    KH = KD // 2
    assert NU == 2 * E
    w_hi, w_lo = t["w_hi"], t["w_lo"]
    with ExitStack() as ctx:
        wo_hi = sb(ctx, "wo_hi", [P, G, D], F32R)
        wo_lo = sb(ctx, "wo_lo", [P, G, D], F32R)
        bo_row = sb(ctx, "bo_row", [P, D], F32)
        spread = sb(ctx, "spread", [2 * H, D], F32R)
        inv_st = sb(ctx, "inv_st", [2 * H, 2, UW], F32R)
        sums = sb(ctx, "sums", [P, 2, G, UW], F32)
        ctx_hi = sb(ctx, "ctx_hi", [P, 2, G, UW], F32R)
        ctx_lo = sb(ctx, "ctx_lo", [P, 2, G, UW], F32R)
        xb = sb(ctx, "xb", [P, X_RING, TPU, D], F32)
        w_raw = sb(ctx, "gu_raw", [P, 2, KH, 2 * F], F32)
        wo_raw = xb[:, 2:4].rearrange("p r j n -> p (r j) n")
        inv, spread_raw = xb[:, 1, 0, :], xb[0:2 * H, 1, 1, :]
        inv_hi, inv_lo = (c[:, 1].rearrange("p g n -> p (g n)")[:, 0:NH * S // P] for c in (ctx_hi, ctx_lo))
        inv_ps = ps(ctx, "inv_ps", [P, 2, G, UW])
        out_ps = ps(ctx, "out_ps", [P, 2, TPU, D])

        small_loaded = sem(ctx, "o_small_loaded")
        wo_loaded = sem(ctx, "wo_loaded")
        lists_loaded = sem(ctx, "lists_loaded")
        wo_hi_ready = sem(ctx, "wo_hi_ready")
        wo_ready = sem(ctx, "wo_ready")
        weight_sums_loaded = sem(ctx, "weight_sums_loaded")
        inverted = sem(ctx, "inverted")
        inv_hi_ready = sem(ctx, "inv_hi_ready")
        inv_ready = sem(ctx, "inv_ready")
        inv_stored = sem(ctx, "inv_stored")
        inv_loaded = [sem(ctx, f"inv_loaded{p}") for p in range(2)]
        sums_loaded = [sem(ctx, f"sums_loaded{p}") for p in range(2)]
        x_loaded = [sem(ctx, f"ox_loaded{p}") for p in range(X_RING)]
        w_loaded = [sem(ctx, f"w_loaded{p}") for p in range(2)]
        w_hi_ready = sem(ctx, "gu_hi_ready")
        w_lo_ready = sem(ctx, "gu_lo_ready")
        spread_ready = sem(ctx, "spread_ready")
        inv_spread = sem(ctx, "inv_spread")
        ctx_ready = sem(ctx, "ctx_ready")
        hi_ready = sem(ctx, "ctx_hi_ready")
        lo_ready = sem(ctx, "ctx_lo_ready")
        xb_ready = sem(ctx, "xb_ready")
        projected = sem(ctx, "projected")
        taken = sem(ctx, "taken")
        stored = [sem(ctx, f"stored{p}") for p in range(X_RING)]
        block = ctx.enter_context(nc.Block())

        @block.sync
        def _(sp):
            rows_of = lambda d: d.rearrange("n (a b) -> (n a) b", b=NH * S // P)

            def columns(u):
                return u // (NU // B), bass.ds((u % (NU // B)) * UW, UW)

            def load_sums(u, par):
                b, at = columns(u)
                sp.dma_start(sums[:, par], t["ctx_d"][bass.ds(b * D, D), at].rearrange("(g p) n -> p g n", p=P)).then_inc(sums_loaded[par], 16)

            def load_inverses(u, par):
                b, at = columns(u)
                for part in range(2):
                    sp.dma_start(inv_st[part * H:(part + 1) * H, par, :].bitcast(F32),
                                 t["inverse_d"][part, bass.ds(b * H, H), at]).then_inc(inv_loaded[par], 16)

            def x_rows(d, u):
                return d[bass.ds(u * UW, UW), :].rearrange("(j p) d -> p j d", p=P)

            def load_x(u, r):
                sp.dma_start(xb[:, r], x_rows(t["x"], u)).then_inc(x_loaded[r], 16)

            def load_weights(e, half):
                for part, name in enumerate(("gate_w", "up_w")):
                    src = t[name][bass.ds(e, 1), half * KH * P:(half + 1) * KH * P, :]
                    sp.dma_start(w_raw[:, half, :, part * F:(part + 1) * F],
                                 src.rearrange("a (k p) f -> p (a k) f", p=P)).then_inc(w_loaded[half], 16)

            sp.dma_start(inv, rows_of(t["weight_sums_d"])).then_inc(weight_sums_loaded, 16)
            sp.dma_start(wo_raw, t["Wo"].rearrange("(g p) n -> p g n", p=P)).then_inc(wo_loaded, 16)
            sp.dma_start(spread_raw, t["spread"]).then_inc(small_loaded, 16)
            sp.dma_start(bo_row[:, :], t["bo"].partition_broadcast(P)).then_inc(small_loaded, 16)
            for u in range(2):
                load_sums(u, u)
            sp.wait_ge(inv_ready, 1)
            for part, src in enumerate((inv_hi, inv_lo)):
                sp.dma_start(rows_of(t["inverse_d"][part]), src.bitcast(F32)).then_inc(inv_stored, 16)
            sp.wait_ge(inv_stored, 32)
            for u in range(2):
                load_inverses(u, u)
            load_x(0, 0)
            for half in range(2):
                load_weights(0, half)
            sp.wait_ge(spread_ready, 1)
            load_x(1, 1)
            sp.wait_ge(wo_ready, 1)
            load_x(2, 2)

            sp.dma_start(t["lists"][:, :, :].rearrange("p n c -> p (n c)"),
                         t["list_d"].rearrange("(p n) c -> p (n c)", p=P)).then_inc(lists_loaded, 16)

            def unit(u, e, r, sums_ahead=True, x_ahead=True):
                if sums_ahead:
                    sp.wait_ge(inv_spread, u + 1)
                    load_inverses(u + 2, r % 2)
                    sp.wait_ge(lo_ready, u + 1)
                    load_sums(u + 2, r % 2)
                    sp.wait_ge(w_lo_ready, u + 1)
                    load_weights(e + 1, r % 2)
                sp.wait_ge(taken, 2 * TPU + TPU * (u + 1))
                sp.dma_start(x_rows(t["out"], u), xb[:, r]).then_inc(stored[r], 16)
                if x_ahead:
                    ahead = (r + X_RING - 1) % X_RING
                    sp.wait_ge(stored[ahead], 16 * ((u + X_RING - 1) // X_RING + 1))
                    load_x(u + X_RING - 1, ahead)

            with nc.sync.Fori(0, NU // X_RING - 1) as i:
                for r in range(X_RING):
                    unit(X_RING * i + r, X_RING // 2 * i + r // 2, r)
            for u in range(NU - X_RING, NU):
                unit(u, u // 2, u % X_RING, sums_ahead=u < NU - 2, x_ahead=u == NU - X_RING)
            for p in range(X_RING):
                sp.wait_ge(stored[p], 16 * (NU // X_RING) + 16)
            sp.wait_ge(lists_loaded, 16)

        @block.gpsimd
        def _(pool):
            pool.wait_ge(small_loaded, 32)

            def add_bias(u, r):
                pool.wait_ge(x_loaded[r], 16 * (u // X_RING + 1))
                for j in range(TPU):
                    nc.gpsimd.tensor_tensor(xb[:, r, j], xb[:, r, j], bo_row[:, :], ALU.add).then_inc(xb_ready, 1)

            def place(w, e, r):
                half = r % 2
                return w[:, bass.ds(e, 1), half * KH:(half + 1) * KH, :].rearrange("p a k f -> p (a k) f")

            with nc.gpsimd.Fori(0, NU // X_RING) as i:
                for r in range(X_RING):
                    u, e = X_RING * i + r, X_RING // 2 * i + r // 2
                    pool.wait_ge(w_hi_ready, u + 1)
                    add_bias(u, r)
                    nc.gpsimd.tensor_tensor(place(w_lo, e, r), w_raw[:, r % 2], place(w_hi, e, r).bitcast(F32),
                                            ALU.subtract).then_inc(w_lo_ready, 1)

        @block.scalar
        def _(act):
            act.sem_inc(projected, 2)
            for p in range(X_RING):
                act.sem_inc(stored[p], 16)
            act.wait_ge(wo_loaded, 16)
            nc.scalar.activation(wo_hi[:, :, :], wo_raw, ACT.Copy).then_inc(wo_hi_ready, 1)

            def high(u, r):
                act.wait_ge(ctx_ready, u + 1)
                act.wait_ge(projected, u + 1)
                nc.scalar.activation(ctx_hi[:, r % 2], sums[:, r % 2], ACT.Copy).then_inc(hi_ready, 1)

            with nc.scalar.Fori(0, NU // X_RING) as i:
                for r in range(X_RING):
                    u, e, half = X_RING * i + r, X_RING // 2 * i + r // 2, r % 2
                    act.wait_ge(w_loaded[half], 32 * (u // 2 + 1))
                    high(u, r)
                    dst = w_hi[:, bass.ds(e, 1), half * KH:(half + 1) * KH, :].rearrange("p a k f -> p (a k) f")
                    nc.scalar.activation(dst, w_raw[:, half], ACT.Copy).then_inc(w_hi_ready, 1)

        @block.vector
        def _(dve):
            V = nc.vector
            dve.sem_inc(taken, 2 * TPU)
            dve.wait_ge(weight_sums_loaded, 16)
            V.reciprocal(inv, inv).then_inc(inverted, 1)
            dve.wait_ge(inverted, 1)
            V.tensor_copy(inv_hi, inv).then_inc(inv_hi_ready, 1)
            dve.wait_ge(inv_hi_ready, 1)
            V.tensor_tensor(inv_lo, inv, inv_hi.bitcast(F32), ALU.subtract).then_inc(inv_ready, 1)
            dve.wait_ge(small_loaded, 32)
            V.tensor_copy(spread[:, :], spread_raw).then_inc(spread_ready, 1)
            dve.wait_ge(wo_hi_ready, 1)
            V.tensor_tensor(wo_lo[:, :, :], wo_raw, wo_hi[:, :, :].bitcast(F32), ALU.subtract).then_inc(wo_ready, 1)

            def context(u, r):
                dve.wait_ge(sums_loaded[r % 2], 16 * (u // 2 + 1))
                dve.wait_ge(inv_spread, u + 1)
                V.tensor_tensor(sums[:, r % 2], sums[:, r % 2], inv_ps[:, r % 2], ALU.mult).then_inc(ctx_ready, 1)
                dve.wait_ge(hi_ready, u + 1)
                V.tensor_tensor(ctx_lo[:, r % 2], sums[:, r % 2], ctx_hi[:, r % 2].bitcast(F32), ALU.subtract).then_inc(lo_ready, 1)

            def take(u, r):
                dve.wait_ge(projected, 2 + u + 1)
                dve.wait_ge(xb_ready, TPU * (u + 1))
                for j in range(TPU):
                    V.tensor_tensor(xb[:, r, j], out_ps[:, r % 2, j], xb[:, r, j], ALU.add).then_inc(taken, 1)

            def unit(u, r, ahead=True):
                if ahead:
                    context(u + 1, r + 1)
                take(u, r)

            context(0, 0)
            with nc.vector.Fori(0, NU // X_RING - 1) as i:
                for r in range(X_RING):
                    unit(X_RING * i + r, r)
            for r in range(X_RING):
                unit(NU - X_RING + r, r, ahead=r < X_RING - 1)

        @block.tensor
        def _(pe):
            def spread_inverses(u, r, first=False):
                pe.wait_ge(inv_loaded[r % 2], 32 * (u // 2 + 1))
                if not first:
                    pe.wait_ge(ctx_ready, u - 1)
                for g in range(G):
                    last = nc.tensor.matmul(inv_ps[:, r % 2, g], spread[:, g * P:(g + 1) * P], inv_st[:, r % 2, :],
                                            start=True, stop=True)
                last.then_inc(inv_spread, 1)

            def project_unit(u, r):
                pe.wait_ge(lo_ready, u + 1)
                pe.wait_ge(taken, TPU * (u + 1))
                for j in range(TPU):
                    rows = slice(j * P, (j + 1) * P)
                    for g in range(G):
                        for n, (lhs, w) in enumerate(((ctx_hi, wo_hi), (ctx_hi, wo_lo), (ctx_lo, wo_hi))):
                            last = nc.tensor.matmul(out_ps[:, r % 2, j], lhs[:, r % 2, g, rows], w[:, g, :],
                                                    start=(g == 0 and n == 0), stop=(g == G - 1 and n == 2))
                last.then_inc(projected, 1)

            pe.wait_ge(spread_ready, 1)
            for u in range(2):
                spread_inverses(u, u, first=True)
            pe.wait_ge(wo_ready, 1)
            with nc.tensor.Fori(0, NU // X_RING - 1) as i:
                for r in range(X_RING):
                    project_unit(X_RING * i + r, r)
                    spread_inverses(X_RING * i + r + 2, r)
            for r in range(X_RING):
                project_unit(NU - X_RING + r, r)
                if r < X_RING - 2:
                    spread_inverses(NU - X_RING + r + 2, r)


def experts(nc, sb, ps, sem, t):
    ident, tile_expert, lists = t["ident"], t["tile_expert"], t["lists"]
    w_hi, w_lo, out = t["w_hi"], t["w_lo"], t["out"]
    with ExitStack() as ctx:
        w_down = sb(ctx, "w_down", [P, E, KF, D], F32)
        row_in = sb(ctx, "row_in", [P, 2], I32)
        row_out = sb(ctx, "row_out", [P, 2], I32)
        share = sb(ctx, "share", [P, 2], F32)
        xg = sb(ctx, "xg", [P, 2, D], F32)
        x_hi = sb(ctx, "ex_hi", [P, 2, KD, P], F32R)
        x_lo = sb(ctx, "ex_lo", [P, 2, KD, P], F32R)
        th = sb(ctx, "th", [P, 2, F], F32)
        gated = sb(ctx, "gated", [P, 2, F], F32)
        inner = sb(ctx, "inner", [P, 2, F], F32)
        inner_t = sb(ctx, "inner_t", [P, 2, KF, P], F32)
        y = sb(ctx, "y", [P, 2, D], F32)
        xt_ps = ps(ctx, "xt_ps", [P, 2, KD, P])
        h_ps = ps(ctx, "h_ps", [P, 2, 2 * F])
        it_ps = ps(ctx, "it_ps", [P, 2, CH])
        y_ps = ps(ctx, "y_ps", [P, 2, D])

        w_down_loaded = sem(ctx, "w_down_loaded")
        held = sem(ctx, "held")
        row_in_ready = sem(ctx, "row_in_ready")
        share_ready = sem(ctx, "share_ready")
        xg_loaded = [sem(ctx, f"xg_loaded{p}") for p in range(2)]
        x_turned = sem(ctx, "x_turned")
        x_hi_ready = sem(ctx, "ex_hi_ready")
        x_lo_ready = sem(ctx, "ex_lo_ready")
        h_ready = sem(ctx, "h_ready")
        th_ready = sem(ctx, "th_ready")
        gated_ready = sem(ctx, "gated_ready")
        inner_ready = sem(ctx, "inner_ready")
        inner_turned = sem(ctx, "inner_turned")
        inner_t_ready = sem(ctx, "inner_t_ready")
        y_made = sem(ctx, "y_made")
        y_scaled = sem(ctx, "y_scaled")
        added = sem(ctx, "added")
        block = ctx.enter_context(nc.Block())

        def over_tiles(engine, step):
            loops = (NMT - 3) // 2
            with engine.Fori(0, loops) as i:
                for p in range(2):
                    step(2 * i + p, p, NMT)
            for tile in range(2 * loops, NMT):
                step(tile, tile % 2, NMT - tile)

        @block.sync
        def _(sp):
            for p in range(2):
                sp.wait_ge(xg_loaded[p], 16)
            for e in range(E):
                sp.dma_start(w_down[:, e], t["down_w"][e].rearrange("(k p) n -> p k n", p=P)).then_inc(w_down_loaded, 16)

        @block.gpsimd
        def _(pool):
            def hold():
                pool.sem_inc(held, 1)

            def fetch(n, p):
                pool.wait_ge(x_turned, n + 1)
                hold()
                nc.gpsimd.tensor_copy(row_in[:, p:p + 1], lists[:, bass.ds(n, 1), 0]).then_inc(row_in_ready, 1)
                pool.wait_ge(row_in_ready, n + 1)
                hold()
                nc.gpsimd.indirect_dma_start(out=xg[:, p, :], out_offset=None, in_=t["xn_d"],
                                             in_offset=bass.IndirectOffsetOnAxis(ap=row_in[:, p:p + 1], axis=0)
                                             ).then_inc(xg_loaded[p], 16)

            def take_shares(n, p):
                nc.gpsimd.tensor_copy(row_out[:, p:p + 1], lists[:, bass.ds(n, 1), 0])
                nc.gpsimd.tensor_copy(share[:, p:p + 1], lists[:, bass.ds(n, 1), 1].bitcast(F32)).then_inc(share_ready, 1)

            def add_rows(n, p):
                pool.wait_ge(share_ready, n + 1)
                pool.wait_ge(y_scaled, 2 + n + 1)
                hold()
                nc.gpsimd.indirect_dma_start(out=out, out_offset=bass.IndirectOffsetOnAxis(ap=row_out[:, p:p + 1], axis=0),
                                             in_=y[:, p, :], in_offset=None, compute_op=ALU.add).then_inc(added, 16)

            pool.sem_inc(x_turned, 2)
            for n in range(2):
                fetch(n, n)
            take_shares(0, 0)
            for n in range(2, 4):
                fetch(n, n % 2)

            def step(n, p, left):
                add_rows(n, p)
                if left > 4:
                    fetch(n + 4, p)
                if left > 1:
                    take_shares(n + 1, 1 - p)
                pool.wait_ge(added, 16 * (n + 1))

            loops = (NMT - 4) // 2
            with nc.gpsimd.Fori(0, loops) as i:
                for p in range(2):
                    step(2 * i + p, p, NMT)
            for n in range(2 * loops, NMT):
                step(n, n % 2, NMT - n)

        @block.scalar
        def _(act):
            def high(n, p):
                act.wait_ge(x_turned, 2 + n + 1)
                act.wait_ge(h_ready, n + 1)
                nc.scalar.activation(x_hi[:, p], xt_ps[:, p], ACT.Copy).then_inc(x_hi_ready, 1)

            def half_tanh(n, p):
                act.wait_ge(h_ready, 2 + n + 1)
                act.wait_ge(inner_ready, n + 1)
                nc.scalar.activation(th[:, p], h_ps[:, p, 0:F], ACT.Tanh, scale=0.5).then_inc(th_ready, 1)

            def scale(n, p):
                act.wait_ge(y_made, 2 + n + 1)
                act.wait_ge(share_ready, n + 1)
                nc.scalar.activation(y[:, p], y_ps[:, p], ACT.Copy, scale=share[:, p:p + 1]).then_inc(y_scaled, 1)

            act.sem_inc(y_scaled, 2)
            high(0, 0)
            high(1, 1)
            half_tanh(0, 0)

            def step(n, p, left):
                if left > 1:
                    half_tanh(n + 1, 1 - p)
                if left > 2:
                    high(n + 2, p)
                scale(n, p)

            over_tiles(nc.scalar, step)

        @block.vector
        def _(dve):
            V = nc.vector

            def low(n, p):
                dve.wait_ge(x_hi_ready, n + 1)
                V.tensor_tensor(x_lo[:, p], xt_ps[:, p], x_hi[:, p].bitcast(F32), ALU.subtract).then_inc(x_lo_ready, 1)

            def gate(n, p):
                dve.wait_ge(th_ready, n + 1)
                V.scalar_tensor_tensor(gated[:, p], th[:, p], 1.0, h_ps[:, p, 0:F], ALU.add, ALU.mult).then_inc(gated_ready, 1)
                dve.wait_ge(gated_ready, n + 1)
                dve.wait_ge(inner_turned, n + 1)
                V.scalar_tensor_tensor(inner[:, p], gated[:, p], 0.5, h_ps[:, p, F:2 * F], ALU.mult, ALU.mult).then_inc(inner_ready, 1)

            def take_turned(n, p):
                dve.wait_ge(inner_turned, 2 + n + 1)
                dve.wait_ge(y_made, n + 1)
                V.tensor_copy(inner_t[:, p], it_ps[:, p, 0:F].rearrange("p (k n) -> p k n", k=KF)).then_inc(inner_t_ready, 1)

            for s in (x_lo_ready, inner_ready, inner_t_ready):
                dve.sem_inc(s, 2)
            low(0, 0)
            low(1, 1)
            gate(0, 0)

            def step(n, p, left):
                take_turned(n, p)
                if left > 1:
                    gate(n + 1, 1 - p)
                if left > 2:
                    low(n + 2, p)

            over_tiles(nc.vector, step)

        @block.tensor
        def _(pe):
            def expert_of(n):
                return pe.value_load(tile_expert[0:1, bass.ds(n, 1)], min_val=0, max_val=E - 1)

            def turn_rows(n, p):
                pe.wait_ge(xg_loaded[p], 16 * (n // 2 + 1))
                pe.wait_ge(x_lo_ready, n + 1)
                for k in range(KD):
                    last = nc.tensor.transpose(xt_ps[:, p, k], xg[:, p, k * P:(k + 1) * P], ident)
                last.then_inc(x_turned, 1)

            def gate_up(n, p):
                e = expert_of(n)
                pe.wait_ge(x_lo_ready, 2 + n + 1)
                pe.wait_ge(inner_ready, n + 1)
                for k in range(KD):
                    for m, (lhs, w) in enumerate(((x_hi, w_hi), (x_hi, w_lo), (x_lo, w_hi))):
                        rhs = w[:, bass.ds(e, 1), k, :].rearrange("p a f -> p (a f)")
                        last = nc.tensor.matmul(h_ps[:, p], lhs[:, p, k], rhs, start=(k == 0 and m == 0),
                                                stop=(k == KD - 1 and m == 2))
                last.then_inc(h_ready, 1)

            def turn_inner(n, p):
                pe.wait_ge(inner_ready, 2 + n + 1)
                pe.wait_ge(inner_t_ready, n + 1)
                for k in range(KF):
                    last = nc.tensor.transpose(it_ps[:, p, k * P:(k + 1) * P], inner[:, p, k * P:(k + 1) * P], ident)
                last.then_inc(inner_turned, 1)

            def down(n, p):
                e = expert_of(n)
                pe.wait_ge(w_down_loaded, 16 * E)
                pe.wait_ge(inner_t_ready, 2 + n + 1)
                pe.wait_ge(y_scaled, n + 1)
                for k in range(KF):
                    rhs = w_down[:, bass.ds(e, 1), k, :].rearrange("p a n -> p (a n)")
                    last = nc.tensor.matmul(y_ps[:, p], inner_t[:, p, k], rhs, start=(k == 0), stop=(k == KF - 1))
                last.then_inc(y_made, 1)

            for s in (h_ready, inner_turned, y_made):
                pe.sem_inc(s, 2)
            turn_rows(0, 0)
            turn_rows(1, 1)
            gate_up(0, 0)

            def step(n, p, left):
                if left > 1:
                    gate_up(n + 1, 1 - p)
                turn_inner(n, p)
                if left > 2:
                    turn_rows(n + 2, p)
                down(n, p)

            over_tiles(nc.tensor, step)


def kernel(**inputs):
    import numpy as np
    import concourse.bacc as bacc
    from concourse.bass_utils import run_bass_kernel_spmd

    pre = {n: np.ascontiguousarray(a) for n, a in inputs.items()}
    i, j = np.arange(P)[:, None], np.arange(P)[None, :]
    f32 = np.float32

    def columns(a):
        return np.ascontiguousarray(a.reshape(KD, P, -1).transpose(1, 0, 2).reshape(P, -1))

    arrays = {
        "x": pre["L0_attn_x"].reshape(T, D),
        "Wq": pre["L0_attn_Wq"], "bq": columns(pre["L0_attn_bq"]), "Wk": pre["L0_attn_Wk"], "bk": columns(pre["L0_attn_bk"]),
        "Wv": pre["L0_attn_Wv"], "bv": pre["L0_attn_bv"], "Wo": pre["L0_attn_Wo"], "bo": pre["L0_attn_bo"],
        "rwT": columns(pre["L0_ffn_router_w"].T), "nw": columns(pre["L0_ffn_norm_w"]),
        "gate_w": pre["L0_ffn_gate_w"], "up_w": pre["L0_ffn_up_w"], "down_w": pre["L0_ffn_down_w"],
        "cst": np.concatenate([i == j, np.where(j <= i, 0.0, NEG), np.where(j >= i, 0.0, NEG), i < j,
                               np.ones((P, P))], axis=1).astype(f32),
        "rows": np.tile(np.concatenate([np.arange(E), P * np.arange(NMT + 1)]).astype(f32), (P, 1)),
        "alibi": ((2.0 ** (-8.0 / H)) ** np.arange(1, H + 1)[:, None] * np.arange(1 - S, 1)[None, :] / SCALE).astype(f32),
        "spread": np.tile(np.arange(H)[:, None] == np.arange(D)[None, :] // HD, (2, 1)).astype(f32),
        "token_pairs": np.stack([np.repeat(i + P * np.arange(TT)[None, :], TOP_K, axis=1),
                                 np.zeros((P, TT * TOP_K))], axis=-1).reshape(P, -1).astype(np.int32),
        "no_pairs": np.stack([T + np.arange(NMT * P) // NMT, np.zeros(NMT * P)], axis=-1).reshape(P, -1).astype(np.int32),
        "no_rows": np.zeros((P, D), f32),
    }
    nc = bacc.Bacc("TRN2", target_bir_lowering=False, num_devices=1)
    args = {n: nc.dram_tensor(f"in_{n}", a.shape, mybir.dt.from_np(a.dtype), kind="ExternalInput").ap()
            for n, a in arrays.items()}
    args["out"] = nc.dram_tensor("out", (T + P, D), F32, kind="ExternalOutput").ap()
    attention_and_experts(nc, **args)
    r = run_bass_kernel_spmd(nc, [{f"in_{n}": a for n, a in arrays.items()}], core_ids=[0])
    return np.asarray(r.results[0]["out"])[:T].reshape(B, S, D)
```
